# Optimizing a Trainium2 kernel written in Bass

```python
import numpy as np
import jax
import jax.numpy as jnp

def _softmax(x, axis=-1):
    return jax.nn.softmax(x, axis=axis)

def _gelu(x):
    return jax.nn.gelu(x, approximate=True)

def _silu(x):
    return jax.nn.silu(x)

def _sigmoid(x):
    return jax.nn.sigmoid(x)

def _layernorm(x, axis=-1, eps=1e-05):
    m = jnp.mean(x, axis=axis, keepdims=True)
    v = jnp.var(x, axis=axis, keepdims=True)
    return (x - m) / jnp.sqrt(v + eps)

def _scatter_add(tgt, idx, src, axis=0):
    return tgt.at[idx].add(src)

def _segment_sum(src, seg, n):
    return jax.ops.segment_sum(src, seg, n)
kernel_name = 'mk_gnn_ffn_d1_gnn_r8_0f1c2a'

def setup_inputs(seed: int=0):
    np.random.seed(seed)
    _w = jnp.asarray

    def _rec_inputs():
        import jax
        import jax.numpy as jnp
        _gk = jax.random.key(seed)
        x = -0.0002117 + 1 * jax.random.normal(jax.random.fold_in(_gk, 1), (6250, 512), jnp.float32)
        src = jax.random.randint(jax.random.fold_in(_gk, 2), (100000,), 0, 6250, jnp.int32)
        dst = jnp.minimum((6250 * jax.random.uniform(jax.random.fold_in(_gk, 3), (100000,)) ** 2.0).astype(jnp.int32), 49999)
        _o = jnp.argsort(dst, stable=True)
        src = src[_o]
        dst = dst[_o]
        return (x, src, dst)
    x, src, dst = _rec_inputs()

    def _L0_gnn_setup():
        import jax, jax.numpy as jnp
        import numpy as np
        N_NODES = 6250
        D_IN = 512
        D_OUT = 512
        N_EDGES = 100000
        key = jax.random.key(seed)
        kx, ke, k1, k2, k3, k4 = jax.random.split(key, 6)
        x = jax.random.normal(kx, (N_NODES, D_IN), dtype=jnp.float32)
        edge_index = jax.random.randint(ke, (2, N_EDGES), 0, N_NODES, dtype=jnp.int64)
        b1lim = 1.0 / np.sqrt(D_IN)
        b2lim = 1.0 / np.sqrt(D_OUT)
        W1 = jax.random.uniform(k1, (D_IN, D_OUT), jnp.float32, -b1lim, b1lim)
        b1 = jax.random.uniform(k2, (D_OUT,), jnp.float32, -b1lim, b1lim)
        W2 = jax.random.uniform(k3, (D_OUT, D_OUT), jnp.float32, -b2lim, b2lim)
        b2 = jax.random.uniform(k4, (D_OUT,), jnp.float32, -b2lim, b2lim)
        return {'x': x, 'edge_index': edge_index, 'W1': W1, 'b1': b1, 'W2': W2, 'b2': b2}
    _L0_gnn_all = _L0_gnn_setup()
    _L0_gnn_in = {k: v for k, v in _L0_gnn_all.items() if k in ('W1', 'b1', 'W2', 'b2')}
    del _L0_gnn_all

    def _L0_ffn_setup():
        import jax, jax.numpy as jnp
        import numpy as np
        B, T, D, F, E, K = (8, 1024, 512, 256, 8, 2)

        def _moe_forward(x, Wr, br, W1, b1, W2, b2):
            Bx, Tx, Dx = x.shape
            xf = x.reshape(-1, Dx)
            logits = xf @ Wr + br
            probs = jax.nn.softmax(logits, axis=-1)
            vals, idx = jax.lax.top_k(probs, K)
            cw = (jax.nn.one_hot(idx, E, dtype=x.dtype) * vals[..., None]).sum(axis=1)

            def body(acc, params):
                W1e, b1e, W2e, b2e, cwe = params
                h = jax.nn.relu(xf @ W1e + b1e)
                y = h @ W2e + b2e
                return (acc + cwe[:, None] * y, None)
            out, _ = jax.lax.scan(body, jnp.zeros_like(xf), (W1, b1, W2, b2, cw.T))
            return out.reshape(Bx, Tx, Dx)
        key = jax.random.key(seed)
        k0, k1, k2, k3 = jax.random.split(key, 4)
        s_d = 1.0 / np.sqrt(D)
        s_f = 1.0 / np.sqrt(F)
        return {'x': jax.random.normal(k0, (B, T, D), jnp.float32), 'Wr': jax.random.uniform(k1, (D, E), jnp.float32, -s_d, s_d), 'br': jnp.zeros((E,), jnp.float32), 'W1': jax.random.uniform(k2, (E, D, F), jnp.float32, -s_d, s_d), 'b1': jnp.zeros((E, F), jnp.float32), 'W2': jax.random.uniform(k3, (E, F, D), jnp.float32, -s_f, s_f), 'b2': jnp.zeros((E, D), jnp.float32)}
    _L0_ffn_all = _L0_ffn_setup()
    _L0_ffn_in = {k: v for k, v in _L0_ffn_all.items() if k in ('Wr', 'br', 'W1', 'b1', 'W2', 'b2')}
    del _L0_ffn_all
    return {'x': x, 'src': src, 'dst': dst, 'L0_gnn_W1': _L0_gnn_in['W1'], 'L0_gnn_b1': _L0_gnn_in['b1'], 'L0_gnn_W2': _L0_gnn_in['W2'], 'L0_gnn_b2': _L0_gnn_in['b2'], 'L0_ffn_Wr': _L0_ffn_in['Wr'], 'L0_ffn_br': _L0_ffn_in['br'], 'L0_ffn_W1': _L0_ffn_in['W1'], 'L0_ffn_b1': _L0_ffn_in['b1'], 'L0_ffn_W2': _L0_ffn_in['W2'], 'L0_ffn_b2': _L0_ffn_in['b2']}

def reference(x, src, dst, L0_gnn_W1, L0_gnn_b1, L0_gnn_W2, L0_gnn_b2, L0_ffn_Wr, L0_ffn_br, L0_ffn_W1, L0_ffn_b1, L0_ffn_W2, L0_ffn_b2):
    import jax
    import jax.numpy as jnp

    def _L0_gnn_ref(x, edge_index, W1, b1, W2, b2):
        import jax, jax.numpy as jnp
        import numpy as np
        N_NODES = 6250
        D_IN = 512
        D_OUT = 512
        N_EDGES = 100000
        src, dst = (edge_index[0], edge_index[1])
        agg = jax.ops.segment_sum(x[src], dst, num_segments=N_NODES)
        h = x + agg
        h = jax.nn.relu(h @ W1 + b1)
        h = h @ W2 + b2
        return jax.nn.relu(h)

    def _L0_ffn_ref(x, Wr, br, W1, b1, W2, b2):
        import jax, jax.numpy as jnp
        import numpy as np
        B, T, D, F, E, K = (8, 1024, 512, 256, 8, 2)

        def _moe_forward(x, Wr, br, W1, b1, W2, b2):
            Bx, Tx, Dx = x.shape
            xf = x.reshape(-1, Dx)
            logits = xf @ Wr + br
            probs = jax.nn.softmax(logits, axis=-1)
            vals, idx = jax.lax.top_k(probs, K)
            cw = (jax.nn.one_hot(idx, E, dtype=x.dtype) * vals[..., None]).sum(axis=1)

            def body(acc, params):
                W1e, b1e, W2e, b2e, cwe = params
                h = jax.nn.relu(xf @ W1e + b1e)
                y = h @ W2e + b2e
                return (acc + cwe[:, None] * y, None)
            out, _ = jax.lax.scan(body, jnp.zeros_like(xf), (W1, b1, W2, b2, cw.T))
            return out.reshape(Bx, Tx, Dx)
        return _moe_forward(x, Wr, br, W1, b1, W2, b2)
    edge_index = jnp.stack([src, dst])
    x = x + _L0_gnn_ref(_layernorm(x, axis=-1), edge_index, L0_gnn_W1, L0_gnn_b1, L0_gnn_W2, L0_gnn_b2)
    x = x + _L0_ffn_ref(_layernorm(x, axis=-1)[None], L0_ffn_Wr, L0_ffn_br, L0_ffn_W1, L0_ffn_b1, L0_ffn_W2, L0_ffn_b2)[0]
    return x

_drawn_inputs = setup_inputs


def setup_inputs(seed=0):
    import zlib

    import numpy as np

    out = dict(_drawn_inputs(seed))
    spreads = {'L0_ffn_br': (0.0, 0.1), 'L0_ffn_b1': (0.0, 0.776), 'L0_ffn_b2': (0.0, 0.302)}
    factors = {'L0_gnn_b1': 8.0, 'L0_gnn_b2': 3.488}
    for name, (base, spread) in spreads.items():
        noise = np.random.default_rng([zlib.crc32(name.encode()), seed]).standard_normal(out[name].shape)
        drawn = base * np.exp(spread * noise) if base else spread * noise
        out[name] = jnp.asarray(drawn.astype(out[name].dtype))
    for name, factor in factors.items():
        out[name] = (out[name] * factor).astype(out[name].dtype)
    return out
```

```python
from contextlib import ExitStack

import concourse.bass as bass
from concourse import mybir

F32 = mybir.dt.float32
F32R = mybir.dt.float32r
I32 = mybir.dt.int32
U32 = mybir.dt.uint32
ALU = mybir.AluOpType
ACT = mybir.ActivationFunctionType
AX_X = mybir.AxisListType.X

P = 128
EPS = 1e-5
TOP = 2
WIN = 96
GT = 4
ST = 4
NOWHERE = 1 << 20


def ceil_div(a, b):
    return -(-a // b)


def inside(k, t, low, high):
    return not isinstance(k, int) or low <= t < high


def run_steps(eng, slots, total, steady_end, body, peel=1):
    blocks = max(steady_end // slots, peel)
    for t in range(min(slots * peel, total)):
        body(t // slots, t % slots)
    if blocks > peel:
        with eng.Fori(peel, blocks) as k:
            for u in range(slots):
                body(k, u)
    for t in range(blocks * slots, total):
        body(t // slots, t % slots)


def back(k, u, d, slots):
    kk, uu = k + (u - d) // slots, (u - d) % slots
    return kk, uu, kk * slots + uu


def stand_for(eng, sem):
    eng.sem_inc(sem, 1)


class Chain:

    def __init__(self, eng, sem, base):
        self.eng, self.sem, self.base, self.n = eng, sem, base, 0

    def link(self, instruction):
        instruction.then_inc(self.sem, 1)
        self.n += 1
        self.eng.wait_ge(self.sem, self.base + self.n)


class Shared:
    pass


def gnn_moe_kernel(nc, x, src, dst, W1, b1, W2, b2, Wr, br, EW1, Eb1, EW2, Eb2, out):
    v = Shared()
    v.x, v.src, v.dst, v.out = x, src, dst, out
    v.W1, v.b1, v.W2, v.b2, v.Wr, v.br = W1, b1, W2, b2, Wr, br
    v.EW1, v.Eb1, v.EW2, v.Eb2 = EW1, Eb1, EW2, Eb2

    v.N, v.D = N, D = x.shape
    v.E = E = src.shape[0]
    v.NX, _, v.F = NX, _, F = EW1.shape
    v.C, v.FC = C, FC = D // P, F // P
    v.NT = NT = ceil_div(N, P)
    v.TAIL = TAIL = N - (NT - 1) * P
    v.NS = NS = ceil_div(NT, ST)
    v.SUP = SUP = ST * P
    v.NC = NC = NT * P + WIN
    v.ROUNDS = ROUNDS = ceil_div(N, WIN)
    v.GE = GE = GT * P
    v.NG = NG = ceil_div(E, GE)
    v.GB = GB = ceil_div(NG, P)
    assert D == 512 and F % P == 0 and NX == 8 and GB == 2 and ROUNDS * WIN <= NC
    assert NT % ST == 1 and NT > 2 * ST

    v.REGION = REGION = ceil_div(N + P, P) * P
    v.STEPS = STEPS = (TOP * N + NX * (P - 1)) // P

    v.normed = nc.dram_tensor("normed_rows", (N, D), F32, kind="Internal").ap()
    v.resid = nc.dram_tensor("residual_rows", (N, D), F32, kind="Internal").ap()
    v.sent = nc.dram_tensor("expert_in_rows", (NX * REGION, D), F32, kind="Internal").ap()
    v.made = nc.dram_tensor("expert_out_rows", (STEPS * P, D), F32, kind="Internal").ap()

    v.rows_of = lambda t: TAIL if isinstance(t, int) and t == NT - 1 else P
    v.tiles_of = lambda s: NT - (NS - 1) * ST if isinstance(s, int) and s == NS - 1 else ST
    v.width_of = lambda s: TAIL if isinstance(s, int) and s == NS - 1 else SUP

    with ExitStack() as whole:
        v.sem = sem = lambda name: whole.enter_context(nc.semaphore(name))
        v.sb = sb = lambda name, shape, dt=F32, ctx=whole: ctx.enter_context(nc.sbuf_tensor(name, shape, dt))
        v.ps = ps = lambda name, shape, dt=F32, ctx=whole: ctx.enter_context(nc.psum_tensor(name, shape, dt))

        v.ident = sb("ident", [P, P])
        v.ones = sb("ones", [P, P])
        v.before = sb("before", [P, P])
        v.eps = sb("eps", [P, 1])
        v.iota8 = sb("iota8", [P, ST, NX])
        v.region_row = sb("region_row", [P, NX])
        v.run_row = sb("run_row", [P, NX])
        v.place = sb("place", [P, NS * ST, TOP])
        v.weight = sb("weight", [P, NS * ST, TOP])

        v.const_ready = sem("const_ready")
        v.mlp_w_in = sem("mlp_w_in")
        v.waits_passed = sem("waits_passed")
        v.dve_waits_passed = sem("dve_waits_passed")

        with ExitStack() as nodes:
            v.node_cols = sb("node_cols", [P, C, NC], ctx=nodes)
            v.w1_sb = sb("w1_sb", [P, C, D], ctx=nodes)
            v.w2_sb = sb("w2_sb", [P, C, D], ctx=nodes)
            v.b1_col = sb("b1_col", [P, C], ctx=nodes)
            v.b2_all = sb("b2_all", [P, D], ctx=nodes)
            v.wr_sb = sb("wr_sb", [P, C, NX], ctx=nodes)
            v.br_all = sb("br_all", [P, ST, NX], ctx=nodes)

            with ExitStack() as edges:
                v.src_t = sb("src_t", [P, GB * P, GT], ctx=edges)
                v.dst_t = sb("dst_t", [P, GB * P, GT], ctx=edges)
                v.low_all = sb("low_all", [P, GB * P], ctx=edges)
                v.low_row = sb("low_row", [1, 2, GB * P], ctx=edges)
                v.low_int = sb("low_int", [1, GB * P], I32, ctx=edges)
                v.wide = sb("wide", [1, 2], ctx=edges)
                v.wide_int = sb("wide_int", [1, 1], I32, ctx=edges)
                v.starts = sb("starts", [P, ROUNDS], ctx=edges)
                v.iota_ps = ps("iota_ps", [P, 512], ctx=edges)

                normalize(nc, v)
                aggregate(nc, v)
            mlp_route(nc, v)
        experts(nc, v)
        combine(nc, v)


def normalize(nc, v):
    N, D, C, NT, NC, GB, E, GE = v.N, v.D, v.C, v.NT, v.NC, v.GB, v.E, v.GE
    sem = v.sem
    SLOTS = 8
    LAG = 2
    full, rest = divmod(E, GE)

    with ExitStack() as ctx:
        def sb(name, shape, dt=F32):
            return v.sb(name, shape, dt, ctx=ctx)

        def ps(name, shape, dt=F32):
            return v.ps(name, shape, dt, ctx=ctx)

        x_in = [sb(f"x_in{i}", [P, D]) for i in range(SLOTS)]
        x_norm = [sb(f"x_norm{i}", [P, D]) for i in range(SLOTS)]
        stats = sb("stats", [P, SLOTS, 6])
        meanvar = sb("meanvar", [P, SLOTS, 2])
        std = sb("std", [P, SLOTS])
        rstd = sb("rstd", [P, SLOTS])
        src_raw = sb("src_raw", [P, GB, GE], I32)
        dst_raw = sb("dst_raw", [P, GB, GE], I32)
        src_f = sb("src_f", [P, GB, GE])
        dst_f = sb("dst_f", [P, GB, GE])
        dst_real = sb("dst_real", [P, GB, GE])
        low = sb("low", [P, GB])
        high = sb("high", [P, GB])
        span = sb("span", [P, GB])
        iota_i = sb("iota_i", [P, WIN], I32)
        start_i = sb("start_i", [P, v.ROUNDS], I32)
        eight_i = sb("eight_i", [P, ST, v.NX], I32)
        region_i = sb("region_i", [P, v.NX], I32)
        turn = [ps(f"turn{i}", [P, C, P]) for i in range(2)]
        turn_edge = [ps(f"turn_edge{i}", [P, GT, P]) for i in range(2)]
        row_ps = ps("row_ps", [P, 2, GB * P])
        low_ps = ps("low_ps", [P, GB * P])

        pads_set = sem("pads_set")
        iotas_made = sem("iotas_made")
        tri_steps = sem("tri_steps")
        edges_in = sem("edges_in")
        edge_chain = sem("edge_chain")
        edges_float = sem("edges_float")
        edge_turned = sem("edge_turned")
        edge_copied = sem("edge_copied")
        rows_turned = sem("rows_turned")
        rows_copied = sem("rows_copied")
        low_spread = sem("low_spread")
        x_loaded = [sem(f"x_loaded{i}") for i in range(SLOTS)]
        x_stored = [sem(f"x_stored{i}") for i in range(SLOTS)]
        norm_chain = sem("norm_chain")
        var_ready = sem("var_ready")
        std_ready = sem("std_ready")
        norm_ready = sem("norm_ready")
        norm_turned = sem("norm_turned")
        cols_copied = sem("cols_copied")

        block = ctx.enter_context(nc.Block())

        @block.sync
        def _(sp):
            def load_x(k, u):
                t = k * SLOTS + u
                r = v.rows_of(t)
                sp.dma_start(x_in[u][0:r, :], v.x[bass.ds(t * P, r), :]).then_inc(x_loaded[u], 16)

            for t in range(SLOTS):
                load_x(0, t)
            sp.wait_ge(pads_set, 2)
            for raw, given in ((src_raw, v.src), (dst_raw, v.dst)):
                for b in range(GB):
                    n = min(full - b * P, P)
                    sp.dma_start(raw[0:n, b, :], given[b * P * GE:(b * P + n) * GE]
                                 .rearrange("(g e) -> g e", e=GE)).then_inc(edges_in, 16)
                if rest:
                    sp.dma_start(raw[full % P:full % P + 1, full // P, 0:rest],
                                 given[full * GE:E].rearrange("(g e) -> g e", g=1)).then_inc(edges_in, 16)

            def step(k, u):
                t = k * SLOTS + u
                r = v.rows_of(t)
                sp.wait_ge(norm_ready, t + 1)
                sp.dma_start(v.normed[bass.ds(t * P, r), :], x_norm[u][0:r, :]).then_inc(x_stored[u], 16)
                if inside(k, t + SLOTS, 0, NT):
                    load_x(k + 1, u)

            run_steps(sp, SLOTS, NT, NT - 1 - SLOTS, step)
            sp.dma_start(v.w1_sb[:, :, :], v.W1.rearrange("(c p) n -> p c n", p=P)).then_inc(v.mlp_w_in, 16)
            sp.dma_start(v.w2_sb[:, :, :], v.W2.rearrange("(c p) n -> p c n", p=P)).then_inc(v.mlp_w_in, 16)
            sp.dma_start(v.wr_sb[:, :, :], v.Wr.rearrange("(c p) n -> p c n", p=P)).then_inc(v.mlp_w_in, 16)
            sp.dma_start(v.b2_all[:, :], v.b2.partition_broadcast(P)).then_inc(v.mlp_w_in, 16)
            for j in range(ST):
                sp.dma_start(v.br_all[:, j, :], v.br.partition_broadcast(P)).then_inc(v.mlp_w_in, 16)
            sp.dma_start(v.b1_col[:, :], v.b1.rearrange("(c p) -> p c", p=P),
                         allow_slow_non_contiguous=True).then_inc(v.mlp_w_in, 16)
            for u in range(SLOTS):
                sp.wait_ge(x_stored[u], 16 * len(range(u, NT, SLOTS)))

        @block.gpsimd
        def _(pool):
            nc.gpsimd.memset(src_raw[:, :, :], 0).then_inc(pads_set, 1)
            nc.gpsimd.memset(dst_raw[:, :, :], NOWHERE).then_inc(pads_set, 1)
            nc.gpsimd.memset(v.ident[:, :], 0.0).then_inc(tri_steps, 1)
            nc.gpsimd.memset(v.before[:, :], 1.0).then_inc(tri_steps, 1)
            nc.gpsimd.memset(v.ones[:, :], 1.0).then_inc(v.const_ready, 1)
            nc.gpsimd.memset(v.eps[:, :], EPS).then_inc(v.const_ready, 1)
            nc.gpsimd.memset(v.node_cols[:, :, N:NC], 0.0).then_inc(v.const_ready, 1)
            pool.wait_ge(tri_steps, 2)
            nc.gpsimd.affine_select(out=v.ident[:, :], in_=v.ident[:, :], compare_op=ALU.not_equal, fill=1.0,
                                    base=0, pattern=[[-1, P]], channel_multiplier=1).then_inc(v.const_ready, 1)
            nc.gpsimd.affine_select(out=v.before[:, :], in_=v.before[:, :], compare_op=ALU.is_gt, fill=0.0,
                                    base=0, pattern=[[1, P]], channel_multiplier=-1).then_inc(v.const_ready, 1)
            nc.gpsimd.iota(iota_i[:, :], pattern=[[1, WIN]], base=0, channel_multiplier=0).then_inc(iotas_made, 1)
            nc.gpsimd.iota(start_i[:, :], pattern=[[WIN, v.ROUNDS]], base=0,
                           channel_multiplier=0).then_inc(iotas_made, 1)
            nc.gpsimd.iota(eight_i[:, :, :], pattern=[[0, ST], [1, v.NX]], base=0,
                           channel_multiplier=0).then_inc(iotas_made, 1)
            nc.gpsimd.iota(region_i[:, :], pattern=[[v.REGION, v.NX]], base=0,
                           channel_multiplier=0).then_inc(iotas_made, 1)

        @block.vector
        def _(dve):
            dve.wait_ge(iotas_made, 4)
            nc.vector.tensor_copy(v.iota_ps[:, 0:WIN], iota_i[:, :]).then_inc(v.const_ready, 1)
            nc.vector.tensor_copy(v.starts[:, :], start_i[:, :]).then_inc(v.const_ready, 1)
            nc.vector.tensor_copy(v.iota8[:, :, :], eight_i[:, :, :]).then_inc(v.const_ready, 1)
            nc.vector.tensor_copy(v.region_row[:, :], region_i[:, :]).then_inc(v.const_ready, 1)
            nc.vector.tensor_copy(v.run_row[:, :], region_i[:, :]).then_inc(v.const_ready, 1)

            dve.wait_ge(edges_in, 16 * 2 * (GB + (rest > 0)))
            nc.vector.tensor_copy(src_f[:, :, :], src_raw[:, :, :]).then_inc(edges_float, 1)
            c = Chain(dve, edge_chain, 0)
            c.link(nc.vector.tensor_copy(dst_f[:, :, :], dst_raw[:, :, :]))
            nc.vector.tensor_reduce(low[:, :], dst_f[:, :, :], AX_X, ALU.min).then_inc(edges_float, 1)
            c.link(nc.vector.scalar_tensor_tensor(out=dst_real[:, :, :], in0=dst_f[:, :, :],
                                                  scalar=float(NOWHERE // 2), in1=dst_f[:, :, :],
                                                  op0=ALU.is_lt, op1=ALU.mult))
            c.link(nc.vector.tensor_reduce(high[:, :], dst_real[:, :, :], AX_X, ALU.max))
            dve.wait_ge(edges_float, 2)
            nc.vector.tensor_tensor(span[:, :], high[:, :], low[:, :], ALU.subtract).then_inc(edges_float, 1)
            for n, (table, b) in enumerate([(tab, b) for tab in (v.src_t, v.dst_t) for b in range(GB)]):
                dve.wait_ge(edge_turned, n + 1)
                nc.vector.tensor_copy(table[:, b * P:(b + 1) * P, :],
                                      turn_edge[n % 2][:, :, :].rearrange("p j g -> p g j")).then_inc(edge_copied, 1)
            dve.wait_ge(rows_turned, 1)
            c.link(nc.vector.tensor_copy(v.low_row[:, :, :], row_ps[0:1, :, :]))
            nc.vector.tensor_copy(v.low_int[:, :], v.low_row[:, 0, :]).then_inc(rows_copied, 1)
            c.link(nc.vector.tensor_reduce(v.wide[:, 0:1], v.low_row[:, 1, :], AX_X, ALU.max))
            nc.vector.tensor_scalar(v.wide_int[:, :], v.wide[:, 0:1], float(WIN), None,
                                    ALU.is_ge).then_inc(rows_copied, 1)
            dve.wait_ge(low_spread, 1)
            nc.vector.tensor_copy(v.low_all[:, :], low_ps[:, :]).then_inc(rows_copied, 1)

            def step(k, u):
                t = k * SLOTS + u
                if inside(k, t, 0, NT):
                    r = v.rows_of(t)
                    dve.wait_ge(x_loaded[u], 16 * (k + 1))
                    if inside(k, t, SLOTS, NT):
                        dve.wait_ge(std_ready, t - SLOTS + 1)
                    nc.vector.bn_stats(stats[0:r, u, :], x_in[u][0:r, :]).then_inc(norm_chain, 1)
                    dve.wait_ge(norm_chain, t + 1)
                    stand_for(dve, v.dve_waits_passed)
                    nc.vector.bn_aggr(meanvar[0:r, u, :], stats[0:r, u, :]).then_inc(var_ready, 1)
                kb, ub, tb = back(k, u, LAG, SLOTS)
                if inside(k, tb, 0, NT):
                    r = v.rows_of(tb)
                    dve.wait_ge(std_ready, tb + 1)
                    nc.vector.reciprocal(rstd[0:r, ub:ub + 1], std[0:r, ub:ub + 1]).then_inc(rstd_ready, 1)
                    dve.wait_ge(rstd_ready, tb + 1)
                    dve.wait_ge(var_ready, tb + 1)
                    if inside(k, tb, SLOTS, NT):
                        dve.wait_ge(x_stored[ub], 16 * kb)
                        dve.wait_ge(norm_turned, tb - SLOTS + 1)
                    nc.vector.tensor_scalar(x_norm[ub][0:r, :], x_in[ub][0:r, :], meanvar[0:r, ub, 0:1],
                                            rstd[0:r, ub:ub + 1], ALU.subtract, ALU.mult).then_inc(norm_ready, 1)

            rstd_ready = v.sem("rstd_ready")
            run_steps(dve, SLOTS, NT + LAG, NT - 1, step, peel=2)

        @block.scalar
        def _(act):
            act.wait_ge(v.const_ready, 10)

            def step(k, u):
                t = k * SLOTS + u
                if inside(k, t, 0, NT):
                    r = v.rows_of(t)
                    act.wait_ge(var_ready, t + 1)
                    if inside(k, t, SLOTS, NT):
                        act.wait_ge(norm_ready, t - SLOTS + 1)
                    nc.scalar.activation(std[0:r, u:u + 1], meanvar[0:r, u, 1:2], ACT.Sqrt,
                                         bias=v.eps[0:r, :]).then_inc(std_ready, 1)
                kb, ub, tb = back(k, u, LAG + 1, SLOTS)
                if inside(k, tb, 0, NT):
                    r = v.rows_of(tb)
                    act.wait_ge(norm_turned, tb + 1)
                    nc.scalar.activation(v.node_cols[:, :, bass.ds(tb * P, r)], turn[ub % 2][:, :, 0:r],
                                         ACT.Copy).then_inc(cols_copied, 1)

            run_steps(act, SLOTS, NT + LAG + 1, NT - 1, step)

        @block.tensor
        def _(pe):
            pe.wait_ge(v.const_ready, 10)
            pe.wait_ge(edges_float, 1)
            pe.wait_ge(edge_chain, 1)
            for n, (table, b) in enumerate([(tab, b) for tab in (src_f, dst_f) for b in range(GB)]):
                if n >= 2:
                    pe.wait_ge(edge_copied, n - 1)
                for j in range(GT):
                    last = nc.tensor.transpose(turn_edge[n % 2][:, j, :], table[:, b, j * P:(j + 1) * P],
                                               v.ident[:, :])
                last.then_inc(edge_turned, 1)
            pe.wait_ge(edges_float, 3)
            for n, col in enumerate((low, span)):
                for b in range(GB):
                    last = nc.tensor.transpose(row_ps[0:1, n, b * P:(b + 1) * P], col[:, b:b + 1], v.ident[:, :])
            last.then_inc(rows_turned, 1)
            pe.wait_ge(edge_chain, 4)
            nc.tensor.matmul(low_ps[:, :], v.ones[0:1, :], v.low_row[0:1, 0, :], start=True,
                             stop=True).then_inc(low_spread, 1)

            def step(k, u):
                t = k * SLOTS + u
                r = v.rows_of(t)
                pe.wait_ge(norm_ready, t + 1)
                if inside(k, t, 2, NT):
                    pe.wait_ge(cols_copied, t - 1)
                for c in range(C):
                    last = nc.tensor.transpose(turn[u % 2][:, c, 0:r], x_norm[u][0:r, c * P:(c + 1) * P],
                                               v.ident[0:r, 0:r])
                last.then_inc(norm_turned, 1)

            run_steps(pe, SLOTS, NT, NT - 1, step)


def aggregate(nc, v):
    D, C, NG, ROUNDS, N = v.D, v.C, v.NG, v.ROUNDS, v.N
    sem = v.sem
    SLOTS = 4
    LAG = 1

    with ExitStack() as ctx:
        edge_rows = [v.sb(f"edge_rows{i}", [P, GT, D], ctx=ctx) for i in range(SLOTS)]
        index = [v.sb(f"index{i}", [P, GT], I32, ctx=ctx) for i in range(SLOTS)]
        hot = [v.sb(f"hot{i}", [P, GT, WIN], ctx=ctx) for i in range(2)]
        sums = [v.ps(f"sums{i}", [P, 512], ctx=ctx) for i in range(2)]

        index_ready = sem("index_ready")
        gathered = [sem(f"gathered{i}") for i in range(SLOTS)]
        hot_ready = sem("hot_ready")
        sums_ready = sem("sums_ready")
        added = sem("added")
        every_index_ready = sem("every_index_ready")
        every_gathered = sem("every_gathered")
        every_hot_ready = sem("every_hot_ready")
        every_sums_ready = sem("every_sums_ready")
        every_added = sem("every_added")

        def sums_of(i):
            return sums[i][:, 0:C * WIN].rearrange("p (c w) -> p c w", c=C)

        def is_wide(eng):
            return eng.value_load(v.wide_int[0:1, 0:1], min_val=0, max_val=1)

        def gather(u, signal):
            for j in range(GT):
                nc.gpsimd.indirect_dma_start(
                    out=edge_rows[u][:, j, :], out_offset=None, in_=v.normed[:, :],
                    in_offset=bass.IndirectOffsetOnAxis(ap=index[u][:, j:j + 1], axis=0)).then_inc(signal, 16)

        def one_hots(h, first, g, signal):
            for j in range(GT):
                last = nc.vector.tensor_scalar(hot[h][:, j, :], v.iota_ps[:, 0:WIN], first,
                                               v.dst_t[:, bass.ds(g, 1), j], ALU.add, ALU.is_equal)
            last.then_inc(signal, 1)

        def products(u, h, signal):
            for c in range(C):
                for j in range(GT):
                    last = nc.tensor.matmul(sums_of(h)[:, c, :], edge_rows[u][:, j, c * P:(c + 1) * P],
                                            hot[h][:, j, :], start=(j == 0), stop=(j == GT - 1))
            last.then_inc(signal, 1)

        def add_window(h, start, signal):
            window = v.node_cols[:, :, bass.ds(start, WIN)]
            nc.vector.tensor_tensor(window, sums_of(h), window, ALU.add).then_inc(signal, 1)

        block = ctx.enter_context(nc.Block())

        @block.scalar
        def _(act):
            def step(k, u):
                t = k * SLOTS + u
                if inside(k, t, SLOTS, NG):
                    act.wait_ge(gathered[u], 16 * GT * k)
                nc.scalar.activation(index[u][:, :], v.src_t[:, bass.ds(t, 1), :].rearrange("p g j -> p (g j)"),
                                     ACT.Copy).then_inc(index_ready, 1)

            def every(g, first):
                if not first:
                    act.wait_ge(every_gathered, 16 * GT * g)
                nc.scalar.activation(index[0][:, :], v.src_t[:, bass.ds(g, 1), :].rearrange("p g j -> p (g j)"),
                                     ACT.Copy).then_inc(every_index_ready, 1)

            wide = is_wide(act)
            with act.If(wide == 0):
                run_steps(act, SLOTS, NG, NG, step)
            with act.Else():
                every(0, True)
                with act.Fori(1, NG) as g:
                    every(g, False)

        @block.gpsimd
        def _(pool):
            def step(k, u):
                t = k * SLOTS + u
                pool.wait_ge(index_ready, t + 1)
                if inside(k, t, SLOTS, NG):
                    pool.wait_ge(sums_ready, t - SLOTS + 1)
                stand_for(pool, v.waits_passed)
                gather(u, gathered[u])

            def every(g, first):
                pool.wait_ge(every_index_ready, g + 1)
                if not first:
                    pool.wait_ge(every_sums_ready, g * ROUNDS)
                stand_for(pool, v.waits_passed)
                gather(0, every_gathered)

            wide = is_wide(pool)
            with pool.If(wide == 0):
                run_steps(pool, SLOTS, NG, NG, step)
            with pool.Else():
                every(0, True)
                with pool.Fori(1, NG) as g:
                    every(g, False)

        @block.vector
        def _(dve):
            def step(k, u):
                t = k * SLOTS + u
                if inside(k, t, 0, NG):
                    if inside(k, t, 2, NG):
                        dve.wait_ge(sums_ready, t - 1)
                    one_hots(u % 2, v.low_all[:, bass.ds(t, 1)], t, hot_ready)
                kb, ub, tb = back(k, u, LAG, SLOTS)
                if inside(k, tb, 0, NG):
                    start = dve.value_load(v.low_int[0:1, bass.ds(tb, 1)], min_val=0, max_val=N - 1)
                    dve.wait_ge(sums_ready, tb + 1)
                    if inside(k, tb, 1, NG):
                        dve.wait_ge(added, tb)
                    add_window(ub % 2, start, added)

            def every(g, first):
                def window(r, first_window):
                    n = g * ROUNDS + r
                    one_hots(0, v.starts[:, bass.ds(r, 1)], g, every_hot_ready)
                    dve.wait_ge(every_sums_ready, n + 1)
                    if not first_window:
                        dve.wait_ge(every_added, n)
                    add_window(0, r * WIN, every_added)

                window(0, first)
                with dve.Fori(1, ROUNDS) as r:
                    window(r, False)

            wide = is_wide(dve)
            with dve.If(wide == 0):
                run_steps(dve, SLOTS, NG + LAG, NG, step)
            with dve.Else():
                every(0, True)
                with dve.Fori(1, NG) as g:
                    every(g, False)

        @block.tensor
        def _(pe):
            def step(k, u):
                t = k * SLOTS + u
                pe.wait_ge(gathered[u], 16 * GT * (k + 1))
                pe.wait_ge(hot_ready, t + 1)
                if inside(k, t, 2, NG):
                    pe.wait_ge(added, t - 1)
                products(u, u % 2, sums_ready)

            def every(g):
                with pe.Fori(0, ROUNDS) as r:
                    pe.wait_ge(every_gathered, 16 * GT * (g + 1))
                    pe.wait_ge(every_hot_ready, g * ROUNDS + r + 1)
                    products(0, 0, every_sums_ready)

            wide = is_wide(pe)
            with pe.If(wide == 0):
                run_steps(pe, SLOTS, NG, NG, step)
            with pe.Else():
                with pe.Fori(0, NG) as g:
                    every(g)


def mlp_route(nc, v):
    N, D, C, NX, NT, NS, SUP = v.N, v.D, v.C, v.NX, v.NT, v.NS, v.SUP
    sem, tiles_of, width_of = v.sem, v.tiles_of, v.width_of
    SLOTS = 2

    with ExitStack() as ctx:
        def sb(name, shape, dt=F32):
            return v.sb(name, shape, dt, ctx=ctx)

        def ps(name, shape, dt=F32):
            return v.ps(name, shape, dt, ctx=ctx)

        x_rows = [sb(f"x_rows{i}", [P, ST, D]) for i in range(SLOTS)]
        x2 = [sb(f"x2_{i}", [P, ST, D]) for i in range(SLOTS)]
        xn = [sb(f"xn_{i}", [P, ST, D]) for i in range(SLOTS)]
        xn_col = [sb(f"xn_col{i}", [P, C, P]) for i in range(2)]
        hidden = sb("hidden", [P, C, SUP])
        stats = sb("stats2", [P, ST, 6])
        meanvar = sb("meanvar2", [P, ST, 2])
        std = sb("std2", [P, ST])
        rstd = sb("rstd2", [P, ST])
        logit = sb("logit", [P, ST, NX])
        peak = sb("peak", [P, ST])
        shifted = sb("shifted", [P, ST, NX])
        expd = sb("expd", [P, ST, NX])
        total = sb("total", [P, ST])
        inverse = sb("inverse", [P, ST])
        prob = sb("prob", [P, ST, NX])
        best = sb("best", [P, ST, NX])
        chosen = sb("chosen", [P, ST, NX], U32)
        chosen_f = sb("chosen_f", [P, ST, NX])
        pick = [sb(f"pick{i}", [P, ST, NX]) for i in range(TOP)]
        picked = sb("picked", [P, ST, NX])
        row_of = sb("row_of", [P, ST, NX])
        row_pick = [sb(f"row_pick{i}", [P, ST, NX]) for i in range(TOP)]
        row_now = sb("row_now", [P, ST, TOP])
        row_int = [sb(f"row_int{i}", [P, TOP, ST], I32) for i in range(SLOTS)]

        hid_ps = [ps(f"hid_ps{i}", [P, SUP]) for i in range(2)]
        out_ps = [ps(f"out_ps{i}", [P, D]) for i in range(2)]
        turn = [ps(f"turn2_{i}", [P, C, P]) for i in range(2)]
        logit_ps = ps("logit_ps", [P, ST, NX])
        rank_ps = ps("rank_ps", [P, 2, ST, NX])

        x_loaded = [sem(f"xr_loaded{i}") for i in range(SLOTS)]
        x2_stored = [sem(f"x2_stored{i}") for i in range(SLOTS)]
        scattered = [sem(f"scattered{i}") for i in range(SLOTS)]
        hid_made = sem("hid_made")
        hid_copied = sem("hid_copied")
        out_made = sem("out_made")
        out_copied = sem("out_copied")
        epi_chain = sem("epi_chain")
        var_ready = sem("var_ready2")
        std_ready = sem("std_ready2")
        rstd_ready = sem("rstd_ready2")
        xn_ready = sem("xn_ready")
        xn_turned = sem("xn_turned")
        xn_copied = sem("xn_copied")
        xn_col_used = sem("xn_col_used")
        shifted_ready = sem("shifted_ready")
        exp_ready = sem("exp_ready")
        route_chain = sem("route_chain")
        picked_ready = sem("picked_ready")
        ranks_ready = sem("ranks_ready")
        place_chain = sem("place_chain")
        place_ready = sem("place_ready")

        def shape_of(s):
            n = tiles_of(s)
            return n, (v.TAIL if n == 1 else P)

        STEPS = NS + 2
        STEADY = NS - 1

        block = ctx.enter_context(nc.Block())

        @block.sync
        def _(sp):
            def rows(dram, s):
                n, r = shape_of(s)
                return dram[bass.ds(s * SUP, width_of(s)), :].rearrange("(j p) d -> p j d", p=r)

            def load(k, u, s):
                n, r = shape_of(s)
                sp.dma_start(x_rows[u][0:r, 0:n, :], rows(v.x, s)).then_inc(x_loaded[u], 16)

            load(0, 0, 0)
            load(0, 1, 1)

            def step(k, u):
                s = k * SLOTS + u
                n, r = shape_of(s)
                sp.wait_ge(var_ready, s * ST + n)
                sp.dma_start(rows(v.resid, s), x2[u][0:r, 0:n, :]).then_inc(x2_stored[u], 16)
                if inside(k, s + SLOTS, 0, NS):
                    nxt = s + SLOTS
                    load(k + 1, u, nxt)

            run_steps(sp, SLOTS, NS, NS - 1 - SLOTS, step)
            for u in range(SLOTS):
                sp.wait_ge(x2_stored[u], 16 * len(range(u, NS, SLOTS)))

        @block.tensor
        def _(pe):
            pe.wait_ge(v.mlp_w_in, 16 * 9)

            def first_layer(s, chunks):
                w = width_of(s)
                for m in chunks:
                    n = s * C + m
                    if inside(s, n, 2, NS * C):
                        pe.wait_ge(hid_copied, n - 1)
                    for c in range(C):
                        last = nc.tensor.matmul(hid_ps[m % 2][:, 0:w], v.w1_sb[:, c, m * P:(m + 1) * P],
                                                v.node_cols[:, c, bass.ds(s * SUP, w)],
                                                start=(c == 0), stop=(c == C - 1))
                    last.then_inc(hid_made, 1)

            def second_layer(s, j):
                _, r = shape_of(s)
                n = s * ST + j
                if j == 0:
                    pe.wait_ge(hid_copied, (s + 1) * C)
                if inside(s, n, 2, NT):
                    pe.wait_ge(out_copied, n - 1)
                for c in range(C):
                    last = nc.tensor.matmul(out_ps[j % 2][0:r, :], hidden[:, c, j * P:j * P + r],
                                            v.w2_sb[:, c, :], start=(c == 0), stop=(c == C - 1))
                last.then_inc(out_made, 1)

            def turn_rows(s, u, j):
                _, r = shape_of(s)
                n = s * ST + j
                pe.wait_ge(xn_ready, n + 1)
                if inside(s, n, 2, NT):
                    pe.wait_ge(xn_copied, n - 1)
                for c in range(C):
                    last = nc.tensor.transpose(turn[j % 2][:, c, 0:r], xn[u][0:r, j, c * P:(c + 1) * P],
                                               v.ident[0:r, 0:r])
                last.then_inc(xn_turned, 1)

            def logits(s, j):
                _, r = shape_of(s)
                n = s * ST + j
                pe.wait_ge(xn_copied, n + 1)
                if j == 0 and inside(s, n, ST, NT):
                    pe.wait_ge(shifted_ready, s)
                for c in range(C):
                    last = nc.tensor.matmul(logit_ps[0:r, j, :], xn_col[j % 2][:, c, 0:r], v.wr_sb[:, c, :],
                                            start=(c == 0), stop=(c == C - 1))
                last.then_inc(xn_col_used, 1)

            def ranks(s):
                n, r = shape_of(s)
                pe.wait_ge(picked_ready, s + 1)
                if inside(s, s, 1, NS):
                    pe.wait_ge(place_ready, s)
                mask = picked[0:r, 0:n, :]
                nc.tensor.matmul(rank_ps[0:r, 0, 0:n, :], v.before[0:r, 0:r], mask, start=True, stop=True)
                nc.tensor.matmul(rank_ps[:, 1, 0:n, :], v.ones[0:r, :], mask, start=True,
                                 stop=True).then_inc(ranks_ready, 1)

            def step(k, u):
                s = k * SLOTS + u
                _, ub, sb_ = back(k, u, 1, SLOTS)
                now, last = inside(k, s, 0, NS), inside(k, sb_, 0, NS)
                if now:
                    first_layer(s, range(C // 2))
                if inside(k, s - 2, 0, NS):
                    ranks(s - 2)
                if now:
                    first_layer(s, range(C // 2, C))
                for j in range(ST):
                    if last and j < tiles_of(sb_):
                        turn_rows(sb_, ub, j)
                    if now and j < tiles_of(s):
                        second_layer(s, j)
                    if last and j < tiles_of(sb_):
                        logits(sb_, j)

            run_steps(pe, SLOTS, STEPS, STEADY, step, peel=2)

        @block.scalar
        def _(act):
            act.wait_ge(v.mlp_w_in, 16 * 9)

            def step(k, u):
                s = k * SLOTS + u
                _, ub, sl = back(k, u, 1, SLOTS)
                if inside(k, s, 0, NS):
                    w = width_of(s)
                    for m in range(C):
                        act.wait_ge(hid_made, s * C + m + 1)
                        if m == 0 and inside(k, s, 1, NS):
                            act.wait_ge(out_made, s * ST)
                        nc.scalar.activation(hidden[:, m, 0:w], hid_ps[m % 2][:, 0:w], ACT.Relu,
                                             bias=v.b1_col[:, m:m + 1]).then_inc(hid_copied, 1)
                if inside(k, sl, 0, NS):
                    n, r = shape_of(sl)
                    for j in range(n):
                        t = sl * ST + j
                        act.wait_ge(xn_turned, t + 1)
                        if inside(k, t, 2, NT):
                            act.wait_ge(xn_col_used, t - 1)
                        nc.scalar.activation(xn_col[j % 2][:, :, 0:r], turn[j % 2][:, :, 0:r],
                                             ACT.Copy).then_inc(xn_copied, 1)
                    act.wait_ge(shifted_ready, sl + 1)
                    nc.scalar.activation(expd[0:r, 0:n, :], shifted[0:r, 0:n, :], ACT.Exp).then_inc(exp_ready, 1)
                if inside(k, s, 0, NS):
                    n, r = shape_of(s)
                    act.wait_ge(var_ready, s * ST + n)
                    if inside(k, s, 1, NS):
                        act.wait_ge(rstd_ready, s)
                    nc.scalar.activation(std[0:r, 0:n], meanvar[0:r, 0:n, 1], ACT.Sqrt,
                                         bias=v.eps[0:r, :]).then_inc(std_ready, 1)

            run_steps(act, SLOTS, NS + 1, STEADY, step)

        @block.vector
        def _(dve):
            dve.wait_ge(v.mlp_w_in, 16 * 9)
            EPI = 2 * ST
            ROUTE = 9
            PLACE = 2 * ST + 2

            def residual(k, u, s):
                n, r = shape_of(s)
                c = Chain(dve, epi_chain, s * EPI)
                dve.wait_ge(x_loaded[u], 16 * (k + 1))
                if inside(k, s, SLOTS, NS):
                    dve.wait_ge(x2_stored[u], 16 * k)
                if inside(k, s, 1, NS):
                    dve.wait_ge(std_ready, s)
                    dve.wait_ge(xn_ready, s * ST)
                for j in range(n):
                    dve.wait_ge(out_made, s * ST + j + 1)
                    rows = x2[u][0:r, j, :]
                    add = nc.vector.tensor_tensor(rows, out_ps[j % 2][0:r, :], v.b2_all[0:r, :], ALU.add)
                    add.then_inc(out_copied, 1)
                    dve.wait_ge(out_copied, s * ST + j + 1)
                    ins = nc.vector.scalar_tensor_tensor(out=rows, in0=rows, scalar=0.0, in1=x_rows[u][0:r, j, :],
                                                         op0=ALU.max, op1=ALU.add)
                    c.link(ins)
                    c.link(nc.vector.bn_stats(stats[0:r, j, :], rows))
                stand_for(dve, v.dve_waits_passed)
                for j in range(n):
                    nc.vector.bn_aggr(meanvar[0:r, j, :], stats[0:r, j, :]).then_inc(var_ready, 1)

            def route(k, s):
                n, r = shape_of(s)
                c = Chain(dve, route_chain, s * ROUTE)

                def wide(t):
                    return t[0:r, 0:n].unsqueeze(2).to_broadcast([r, n, NX])

                dve.wait_ge(xn_col_used, s * ST + n)
                c.link(nc.vector.tensor_tensor(logit[0:r, 0:n, :], logit_ps[0:r, 0:n, :], v.br_all[0:r, 0:n, :],
                                               ALU.add))
                c.link(nc.vector.tensor_reduce(peak[0:r, 0:n], logit[0:r, 0:n, :], AX_X, ALU.max))
                if inside(k, s, 1, NS):
                    dve.wait_ge(exp_ready, s)
                nc.vector.tensor_tensor(shifted[0:r, 0:n, :], logit[0:r, 0:n, :], wide(peak),
                                        ALU.subtract).then_inc(shifted_ready, 1)
                dve.wait_ge(exp_ready, s + 1)
                c.link(nc.vector.tensor_reduce(total[0:r, 0:n], expd[0:r, 0:n, :], AX_X, ALU.add))
                c.link(nc.vector.reciprocal(inverse[0:r, 0:n], total[0:r, 0:n]))
                c.link(nc.vector.tensor_tensor(prob[0:r, 0:n, :], expd[0:r, 0:n, :], wide(inverse), ALU.mult))
                stand_for(dve, v.dve_waits_passed)
                for j in range(n):
                    nc.vector.max(best[0:r, j, :], prob[0:r, j, :]).then_inc(best_ready, 1)
                dve.wait_ge(best_ready, s * ST + n)
                stand_for(dve, v.dve_waits_passed)
                for j in range(n):
                    nc.vector.max_index(chosen[0:r, j, :], best[0:r, j, :],
                                        prob[0:r, j, :]).then_inc(chosen_ready, 1)
                dve.wait_ge(chosen_ready, s * ST + n)
                c.link(nc.vector.tensor_copy(v.weight[0:r, bass.ds(s * ST, n), :], best[0:r, 0:n, 0:TOP]))
                c.link(nc.vector.tensor_copy(chosen_f[0:r, 0:n, :], chosen[0:r, 0:n, :]))
                for i in range(TOP):
                    c.link(nc.vector.tensor_tensor(
                        pick[i][0:r, 0:n, :], v.iota8[0:r, 0:n, :],
                        chosen_f[0:r, 0:n, i].unsqueeze(2).to_broadcast([r, n, NX]), ALU.is_equal))
                nc.vector.tensor_tensor(picked[0:r, 0:n, :], pick[0][0:r, 0:n, :], pick[1][0:r, 0:n, :],
                                        ALU.add).then_inc(picked_ready, 1)
                assert c.n == ROUTE

            def norm(k, u, s):
                n, r = shape_of(s)
                dve.wait_ge(std_ready, s + 1)
                nc.vector.reciprocal(rstd[0:r, 0:n], std[0:r, 0:n]).then_inc(rstd_ready, 1)
                dve.wait_ge(rstd_ready, s + 1)
                if inside(k, s, SLOTS, NS):
                    dve.wait_ge(scattered[u], 16 * TOP * ST * k)
                for j in range(n):
                    nc.vector.tensor_scalar(xn[u][0:r, j, :], x2[u][0:r, j, :], meanvar[0:r, j, 0:1],
                                            rstd[0:r, j:j + 1], ALU.subtract, ALU.mult).then_inc(xn_ready, 1)

            def rows_for(k, u, s):
                n, r = shape_of(s)
                c = Chain(dve, place_chain, s * PLACE)
                dve.wait_ge(ranks_ready, s + 1)
                for j in range(n):
                    c.link(nc.vector.tensor_tensor(row_of[0:r, j, :], rank_ps[0:r, 0, j, :], v.run_row[0:r, :],
                                                   ALU.add))
                    c.link(nc.vector.tensor_tensor(v.run_row[:, :], rank_ps[:, 1, j, :], v.run_row[:, :], ALU.add))
                if inside(k, s, SLOTS, NS):
                    dve.wait_ge(scattered[u], 16 * TOP * ST * k)
                for i in range(TOP):
                    nc.vector.tensor_tensor(row_pick[i][0:r, 0:n, :], pick[i][0:r, 0:n, :], row_of[0:r, 0:n, :],
                                            ALU.mult).then_inc(pick_mult, 1)
                dve.wait_ge(pick_mult, TOP * (s + 1))
                for i in range(TOP):
                    c.link(nc.vector.tensor_reduce(row_now[0:r, 0:n, i], row_pick[i][0:r, 0:n, :], AX_X, ALU.add))
                nc.vector.tensor_copy(v.place[0:r, bass.ds(s * ST, n), :],
                                      row_now[0:r, 0:n, :]).then_inc(place_kept, 1)
                nc.vector.tensor_copy(row_int[u][0:r, :, 0:n],
                                      row_now[0:r, 0:n, :].rearrange("p j i -> p i j")).then_inc(place_ready, 1)
                dve.wait_ge(place_ready, s + 1)

            def step(k, u):
                s = k * SLOTS + u
                kb, ub, sl = back(k, u, 1, SLOTS)
                now, last = inside(k, s, 0, NS), inside(k, sl, 0, NS)
                if inside(k, s - 2, 0, NS):
                    rows_for(k - 1, u, s - 2)
                if now:
                    residual(k, u, s)
                if last:
                    route(kb, sl)
                if now:
                    norm(k, u, s)

            pick_mult = v.sem("pick_mult")
            best_ready = v.sem("best_ready")
            chosen_ready = v.sem("chosen_ready")
            place_kept = v.sem("place_kept")
            run_steps(dve, SLOTS, STEPS, STEADY, step, peel=2)

        @block.gpsimd
        def _(pool):
            def step(k, u):
                s = k * SLOTS + u
                n, r = shape_of(s)
                pool.wait_ge(place_ready, s + 1)
                pool.wait_ge(xn_ready, s * ST + n)
                stand_for(pool, v.waits_passed)
                for j in range(n):
                    for i in range(TOP):
                        nc.gpsimd.indirect_dma_start(
                            out=v.sent[:, :],
                            out_offset=bass.IndirectOffsetOnAxis(ap=row_int[u][0:r, i, j:j + 1], axis=0),
                            in_=xn[u][0:r, j, :], in_offset=None).then_inc(scattered[u], 16)

            run_steps(pool, SLOTS, NS, NS - 1, step)
            for u in range(SLOTS):
                pool.wait_ge(scattered[u], 16 * TOP * sum(tiles_of(s) for s in range(u, NS, SLOTS)))


def experts(nc, v):
    N, D, F, FC, C, NX, STEPS, REGION = v.N, v.D, v.F, v.FC, v.C, v.NX, v.STEPS, v.REGION
    sem = v.sem
    SLOTS = 4

    with ExitStack() as ctx:
        def sb(name, shape, dt=F32):
            return v.sb(name, shape, dt, ctx=ctx)

        w1 = [sb(f"expert_w1_{i}", [P, NX * C * F], F32R) for i in range(2)]
        w2 = [sb(f"expert_w2_{i}", [P, NX * FC * D], F32R) for i in range(2)]
        w1_raw = sb("expert_w1_raw", [P, C * F])
        w2_raw = sb("expert_w2_raw", [P, FC * D])
        bias1 = sb("expert_b1", [P, NX * F])
        bias2 = sb("expert_b2", [P, NX * D])
        zeros = sb("zeros", [P, D])
        rows_in = [sb(f"rows_in{i}", [P, D]) for i in range(SLOTS)]
        cols_in = [[sb(f"cols_in{i}_{h}", [P, C, P], F32R) for h in range(2)] for i in range(2)]
        hid = [sb(f"hid{i}", [P, F]) for i in range(2)]
        hid_col = [[sb(f"hid_col{i}_{h}", [P, FC, P], F32R) for h in range(2)] for i in range(2)]
        rows_out = [sb(f"rows_out{i}", [P, D]) for i in range(SLOTS)]

        count = sb("count", [P, NX])
        tiles_i = sb("tiles_i", [P, NX], I32)
        tiles_s = sb("tiles_s", [P, NX], I32)
        tiles = sb("tiles", [P, NX])
        ends = sb("ends", [P, NX])
        shift = sb("shift", [P, NX])
        shift_more = sb("shift_more", [P, NX])
        later = sb("later", [P, TOP * v.NT])
        place_shift = sb("place_shift", [P, TOP * v.NT])
        tail_i = sb("tail_i", [1, NX], I32)
        step_i = sb("step_i", [1, STEPS], I32)
        step_f = sb("step_f", [1, STEPS])
        past = sb("past", [1, STEPS])
        which = sb("which", [1, STEPS])
        first = sb("first", [1, STEPS])
        within = sb("within", [1, STEPS])
        row_f = sb("row_f", [1, STEPS])
        real = sb("real", [1, STEPS])
        from_f = sb("from_f", [1, STEPS])
        which_f = sb("which_f", [1, STEPS])
        from_row = sb("from_row", [1, STEPS], I32)
        expert = sb("expert", [1, STEPS], I32)

        cols_ps = [v.ps(f"cols_ps{i}", [P, C, P], ctx=ctx) for i in range(2)]
        hid_ps = [v.ps(f"ehid_ps{i}", [P, 512], ctx=ctx) for i in range(2)]
        hcol_ps = [v.ps(f"hcol_ps{i}", [P, 4, P], ctx=ctx) for i in range(2)]
        out_ps = [v.ps(f"eout_ps{i}", [P, D], ctx=ctx) for i in range(2)]

        weights_in = sem("expert_weights_in")
        biases_in = sem("expert_biases_in")
        high_made = sem("expert_high_made")
        weights_ready = sem("expert_weights_ready")
        cols_low_ready = sem("cols_low_ready")
        hcol_low_ready = sem("hcol_low_ready")
        table_chain = sem("table_chain")
        steps_made = sem("steps_made")
        tails_ready = sem("tails_ready")
        table_ready = sem("table_ready")
        zeros_ready = sem("zeros_ready")
        tails_stored = sem("tails_stored")
        rows_loaded = [sem(f"rows_loaded{i}") for i in range(SLOTS)]
        rows_turned = sem("erows_turned")
        cols_ready = sem("cols_ready")
        hid_made = sem("ehid_made")
        hid_ready = sem("ehid_ready")
        hid_turned = sem("ehid_turned")
        hcol_ready = sem("hcol_ready")
        out_made = sem("eout_made")
        out_ready = sem("eout_ready")
        out_stored = [sem(f"eout_stored{i}") for i in range(SLOTS)]

        block = ctx.enter_context(nc.Block())

        @block.sync
        def _(sp):
            sp.wait_ge(tails_ready, 1)
            sp.wait_ge(zeros_ready, 1)
            for e in range(NX):
                row = sp.value_load(tail_i[0:1, e:e + 1], min_val=0, max_val=NX * REGION - P)
                sp.dma_start(v.sent[bass.ds(row, P), :], zeros[:, :]).then_inc(tails_stored, 16)
            sp.wait_ge(table_ready, 2)
            sp.wait_ge(tails_stored, 16 * NX)

            def step(k, u):
                t = k * SLOTS + u
                if inside(k, t, 0, STEPS):
                    if inside(k, t, SLOTS, STEPS):
                        sp.wait_ge(rows_turned, t - SLOTS + 1)
                    row = sp.value_load(from_row[0:1, bass.ds(t, 1)], min_val=0, max_val=NX * REGION - P)
                    sp.dma_start(rows_in[u][:, :], v.sent[bass.ds(row, P), :]).then_inc(rows_loaded[u], 16)

            run_steps(sp, SLOTS, STEPS, STEPS, step)
            for u in range(SLOTS):
                sp.wait_ge(out_stored[u], 16 * len(range(u, STEPS, SLOTS)))

        @block.gpsimd
        def _(pool):
            nc.gpsimd.memset(zeros[:, :], 0.0).then_inc(zeros_ready, 1)
            nc.gpsimd.iota(step_i[:, :], pattern=[[1, STEPS]], base=0, channel_multiplier=0).then_inc(steps_made, 1)
            parts = ((w1, C * F, w1_raw, v.EW1, C), (w2, FC * D, w2_raw, v.EW2, FC))
            for e in range(NX):
                for w, n, raw, given, chunks in parts:
                    pool.dma_start(raw[:, :].rearrange("p (c n) -> p c n", c=chunks),
                                   given[e].rearrange("(c p) n -> p c n", p=P)).then_inc(weights_in, 16)
                pool.wait_ge(weights_in, 16 * 2 * (e + 1))
                if e > 0:
                    for w, n, raw, given, chunks in parts:
                        nc.gpsimd.tensor_copy(w[0][:, e * n:(e + 1) * n], raw[:, :]).then_inc(high_made, 1)
                pool.wait_ge(high_made, 2 * (e + 1))
                for w, n, raw, given, chunks in parts:
                    last = nc.gpsimd.tensor_tensor(w[1][:, e * n:(e + 1) * n], raw[:, :],
                                                   w[0][:, e * n:(e + 1) * n].bitcast(F32), ALU.subtract)
                last.then_inc(weights_ready, 1)
                pool.wait_ge(weights_ready, e + 1)

        @block.scalar
        def _(act):
            act.wait_ge(weights_in, 16 * 2)
            for w, n, raw in ((w1, C * F, w1_raw), (w2, FC * D, w2_raw)):
                nc.scalar.activation(w[0][:, 0:n], raw[:, :], ACT.Copy).then_inc(high_made, 1)
            act.dma_start(bias1[:, :], v.Eb1.rearrange("e f -> (e f)").partition_broadcast(P)).then_inc(biases_in, 16)
            act.dma_start(bias2[:, :], v.Eb2.rearrange("e d -> (e d)").partition_broadcast(P)).then_inc(biases_in, 16)

            def step(k, u):
                t = k * SLOTS + u
                if inside(k, t, 0, STEPS):
                    act.wait_ge(rows_turned, t + 1)
                    if inside(k, t, 2, STEPS):
                        act.wait_ge(hid_made, t - 1)
                    nc.scalar.activation(cols_in[u % 2][0][:, :, :], cols_ps[u % 2][:, :, :],
                                         ACT.Copy).then_inc(cols_ready, 1)
                _, ub, tb = back(k, u, 2, SLOTS)
                if inside(k, tb, 0, STEPS):
                    act.wait_ge(hid_turned, tb + 1)
                    if inside(k, tb, 2, STEPS):
                        act.wait_ge(out_made, tb - 1)
                    nc.scalar.activation(hid_col[ub % 2][0][:, :, :], hcol_ps[ub % 2][:, 0:FC, :],
                                         ACT.Relu).then_inc(hcol_ready, 1)
                _, ub, tb = back(k, u, 3, SLOTS)
                if inside(k, tb, 0, STEPS):
                    act.wait_ge(out_ready, tb + 1)
                    act.dma_start(v.made[bass.ds(tb * P, P), :], rows_out[ub][:, :]).then_inc(out_stored[ub], 16)

            run_steps(act, SLOTS, STEPS + 3, STEPS, step)

        @block.vector
        def _(dve):
            c = Chain(dve, table_chain, 0)
            nc.vector.tensor_copy(tail_i[:, :], v.run_row[0:1, :]).then_inc(tails_ready, 1)
            c.link(nc.vector.tensor_tensor(count[:, :], v.run_row[:, :], v.region_row[:, :], ALU.subtract))
            c.link(nc.vector.tensor_scalar(tiles_i[:, :], count[:, :], float(P - 1), None, ALU.add))
            c.link(nc.vector.tensor_scalar(tiles_s[:, :], tiles_i[:, :], P.bit_length() - 1, None,
                                           ALU.arith_shift_right))
            c.link(nc.vector.tensor_copy(tiles[:, :], tiles_s[:, :]))
            c.link(nc.vector.tensor_copy(ends[:, :], tiles[:, :]))
            for e in range(1, NX):
                c.link(nc.vector.tensor_tensor(ends[:, e:e + 1], ends[:, e - 1:e], tiles[:, e:e + 1], ALU.add))
            c.link(nc.vector.tensor_tensor(shift[:, :], ends[:, :], tiles[:, :], ALU.subtract))
            c.link(nc.vector.scalar_tensor_tensor(out=shift[:, :], in0=shift[:, :], scalar=float(P),
                                                  in1=v.region_row[:, :], op0=ALU.mult, op1=ALU.subtract))
            c.link(nc.vector.tensor_tensor(shift_more[:, 1:], shift[:, 1:], shift[:, 0:NX - 1], ALU.subtract))
            dve.wait_ge(steps_made, 1)
            c.link(nc.vector.tensor_copy(step_f[:, :], step_i[:, :]))
            c.link(nc.vector.tensor_scalar(which[:, :], step_f[:, :], ends[0:1, 0:1], None, ALU.is_ge))
            c.link(nc.vector.tensor_scalar(first[:, :], which[:, :], tiles[0:1, 0:1], None, ALU.mult))
            for e in range(1, NX):
                c.link(nc.vector.tensor_scalar(past[:, :], step_f[:, :], ends[0:1, e:e + 1], None, ALU.is_ge))
                c.link(nc.vector.tensor_tensor(which[:, :], which[:, :], past[:, :], ALU.add))
                c.link(nc.vector.scalar_tensor_tensor(out=first[:, :], in0=past[:, :], scalar=tiles[0:1, e:e + 1],
                                                      in1=first[:, :], op0=ALU.mult, op1=ALU.add))
            c.link(nc.vector.tensor_tensor(within[:, :], step_f[:, :], first[:, :], ALU.subtract))
            c.link(nc.vector.tensor_scalar(row_f[:, :], which[:, :], float(REGION), None, ALU.mult))
            c.link(nc.vector.scalar_tensor_tensor(out=row_f[:, :], in0=within[:, :], scalar=float(P),
                                                  in1=row_f[:, :], op0=ALU.mult, op1=ALU.add))
            c.link(nc.vector.tensor_scalar(real[:, :], which[:, :], float(NX), None, ALU.is_lt))
            c.link(nc.vector.tensor_tensor(from_f[:, :], row_f[:, :], real[:, :], ALU.mult))
            c.link(nc.vector.tensor_tensor(which_f[:, :], which[:, :], real[:, :], ALU.mult))
            nc.vector.tensor_copy(from_row[:, :], from_f[:, :]).then_inc(table_ready, 1)
            nc.vector.tensor_copy(expert[:, :], which_f[:, :]).then_inc(table_ready, 1)
            for rows, tiles_from, tiles_to in ((P, 0, v.NT - 1), (v.TAIL, v.NT - 1, v.NT)):
                lo, hi = TOP * tiles_from, TOP * tiles_to
                place = v.place[0:rows, tiles_from:tiles_to, :].rearrange("p t i -> p (t i)")
                moved = place_shift[0:rows, lo:hi]
                c.link(nc.vector.tensor_scalar(moved, place, 0.0, shift[0:rows, 0:1], ALU.is_ge, ALU.mult))
                for e in range(1, NX):
                    step_by = later[0:rows, lo:hi]
                    c.link(nc.vector.tensor_scalar(step_by, place, float(e * REGION), shift_more[0:rows, e:e + 1],
                                                   ALU.is_ge, ALU.mult))
                    c.link(nc.vector.tensor_tensor(moved, moved, step_by, ALU.add))
                c.link(nc.vector.tensor_tensor(place, place, moved, ALU.add))
            dve.wait_ge(table_ready, 2)
            dve.wait_ge(biases_in, 32)

            def expert_at(t):
                return dve.value_load(expert[0:1, bass.ds(t, 1)], min_val=0, max_val=NX - 1)

            def step(k, u):
                t = k * SLOTS + u
                if inside(k, t, 0, STEPS):
                    dve.wait_ge(cols_ready, t + 1)
                    nc.vector.tensor_tensor(cols_in[u % 2][1][:, :, :], cols_ps[u % 2][:, :, :],
                                            cols_in[u % 2][0][:, :, :].bitcast(F32),
                                            ALU.subtract).then_inc(cols_low_ready, 1)
                kb, ub, tb = back(k, u, 2, SLOTS)
                if inside(k, tb, 0, STEPS):
                    dve.wait_ge(hcol_ready, tb + 1)
                    nc.vector.scalar_tensor_tensor(out=hid_col[ub % 2][1][:, :, :], in0=hcol_ps[ub % 2][:, 0:FC, :],
                                                   scalar=0.0, in1=hid_col[ub % 2][0][:, :, :].bitcast(F32),
                                                   op0=ALU.max, op1=ALU.subtract).then_inc(hcol_low_ready, 1)
                kb, ub, tb = back(k, u, 1, SLOTS)
                if inside(k, tb, 0, STEPS):
                    e = expert_at(tb)
                    dve.wait_ge(hid_made, tb + 1)
                    if inside(k, tb, 2, STEPS):
                        dve.wait_ge(hid_turned, tb - 1)
                    nc.vector.tensor_tensor(hid[ub % 2][:, :], hid_ps[ub % 2][:, 0:F], bias1[:, bass.ds(e * F, F)],
                                            ALU.add).then_inc(hid_ready, 1)
                kb, ub, tb = back(k, u, 2, SLOTS)
                if inside(k, tb, 0, STEPS):
                    e = expert_at(tb)
                    dve.wait_ge(out_made, tb + 1)
                    if inside(k, tb, SLOTS, STEPS):
                        dve.wait_ge(out_stored[ub], 16 * kb)
                    nc.vector.tensor_tensor(rows_out[ub][:, :], out_ps[ub % 2][:, :], bias2[:, bass.ds(e * D, D)],
                                            ALU.add).then_inc(out_ready, 1)

            run_steps(dve, SLOTS, STEPS + 2, STEPS, step, peel=2)

        @block.tensor
        def _(pe):
            pe.wait_ge(table_ready, 2)

            def expert_at(t):
                return pe.value_load(expert[0:1, bass.ds(t, 1)], min_val=0, max_val=NX - 1)

            def three_products(to, cols, w, e, chunks, n):
                passes = [(c, a, b) for c in range(chunks) for a, b in ((0, 0), (0, 1), (1, 0))]
                for i, (c, a, b) in enumerate(passes):
                    last = nc.tensor.matmul(to, cols[a][:, c, :], w[b][:, bass.ds(e * (chunks * n) + c * n, n)],
                                            start=(i == 0), stop=(i == len(passes) - 1))
                return last

            def step(k, u):
                t = k * SLOTS + u
                if inside(k, t, 0, STEPS):
                    pe.wait_ge(rows_loaded[u], 16 * (k + 1))
                    if inside(k, t, 2, STEPS):
                        pe.wait_ge(cols_low_ready, t - 1)
                    for c in range(C):
                        last = nc.tensor.transpose(cols_ps[u % 2][:, c, :], rows_in[u][:, c * P:(c + 1) * P],
                                                   v.ident[:, :])
                    last.then_inc(rows_turned, 1)
                _, ub, tb = back(k, u, 2, SLOTS)
                if inside(k, tb, 0, STEPS):
                    pe.wait_ge(hid_ready, tb + 1)
                    if inside(k, tb, 2, STEPS):
                        pe.wait_ge(hcol_low_ready, tb - 1)
                    for c in range(FC):
                        last = nc.tensor.transpose(hcol_ps[ub % 2][:, c, :], hid[ub % 2][:, c * P:(c + 1) * P],
                                                   v.ident[:, :])
                    last.then_inc(hid_turned, 1)
                _, ub, tb = back(k, u, 1, SLOTS)
                if inside(k, tb, 0, STEPS):
                    e = expert_at(tb)
                    pe.wait_ge(weights_ready, e + 1)
                    pe.wait_ge(cols_low_ready, tb + 1)
                    if inside(k, tb, 2, STEPS):
                        pe.wait_ge(hid_ready, tb - 1)
                    three_products(hid_ps[ub % 2][:, 0:F], cols_in[ub % 2], w1, e, C, F).then_inc(hid_made, 1)
                _, ub, tb = back(k, u, 2, SLOTS)
                if inside(k, tb, 0, STEPS):
                    e = expert_at(tb)
                    pe.wait_ge(hcol_low_ready, tb + 1)
                    if inside(k, tb, 2, STEPS):
                        pe.wait_ge(out_ready, tb - 1)
                    three_products(out_ps[ub % 2][:, :], hid_col[ub % 2], w2, e, FC, D).then_inc(out_made, 1)

            run_steps(pe, SLOTS, STEPS + 2, STEPS, step)


def combine(nc, v):
    N, D, NT = v.N, v.D, v.NT
    sem = v.sem
    SLOTS = 4

    with ExitStack() as ctx:
        def sb(name, shape, dt=F32):
            return v.sb(name, shape, dt, ctx=ctx)

        x2 = [sb(f"x2_in{i}", [P, D]) for i in range(SLOTS)]
        got = [sb(f"got{i}", [P, TOP, D]) for i in range(SLOTS)]
        one = [sb(f"one{i}", [P, D]) for i in range(2)]
        final = [sb(f"final{i}", [P, D]) for i in range(SLOTS)]
        index = [sb(f"place_int{i}", [P, TOP], I32) for i in range(SLOTS)]

        x2_loaded = [sem(f"x2_loaded{i}") for i in range(SLOTS)]
        index_ready = sem("place_int_ready")
        fetched = [sem(f"fetched{i}") for i in range(SLOTS)]
        one_ready = sem("one_ready")
        final_ready = sem("final_ready")
        out_stored = [sem(f"out_stored{i}") for i in range(SLOTS)]

        block = ctx.enter_context(nc.Block())

        @block.sync
        def _(sp):
            def load(k, u, t):
                r = v.rows_of(t)
                sp.dma_start(x2[u][0:r, :], v.resid[bass.ds(t * P, r), :]).then_inc(x2_loaded[u], 16)

            for t in range(SLOTS):
                load(0, t, t)

            def step(k, u):
                t = k * SLOTS + u
                r = v.rows_of(t)
                sp.wait_ge(final_ready, t + 1)
                sp.dma_start(v.out[bass.ds(t * P, r), :], final[u][0:r, :]).then_inc(out_stored[u], 16)
                if inside(k, t + SLOTS, 0, NT):
                    load(k + 1, u, t + SLOTS)

            run_steps(sp, SLOTS, NT, NT - 1 - SLOTS, step)
            for u in range(SLOTS):
                sp.wait_ge(out_stored[u], 16 * len(range(u, NT, SLOTS)))

        @block.scalar
        def _(act):
            def step(k, u):
                t = k * SLOTS + u
                r = v.rows_of(t)
                if inside(k, t, SLOTS, NT):
                    act.wait_ge(fetched[u], 16 * TOP * k)
                nc.scalar.activation(index[u][0:r, :], v.place[0:r, bass.ds(t, 1), :].rearrange("p t i -> p (t i)"),
                                     ACT.Copy).then_inc(index_ready, 1)

            run_steps(act, SLOTS, NT, NT - 1, step)

        @block.gpsimd
        def _(pool):
            def step(k, u):
                t = k * SLOTS + u
                r = v.rows_of(t)
                pool.wait_ge(index_ready, t + 1)
                if inside(k, t, SLOTS, NT):
                    pool.wait_ge(final_ready, t - SLOTS + 1)
                stand_for(pool, v.waits_passed)
                for i in range(TOP):
                    nc.gpsimd.indirect_dma_start(
                        out=got[u][0:r, i, :], out_offset=None, in_=v.made[:, :],
                        in_offset=bass.IndirectOffsetOnAxis(ap=index[u][0:r, i:i + 1], axis=0)
                    ).then_inc(fetched[u], 16)

            run_steps(pool, SLOTS, NT, NT - 1, step)

        @block.vector
        def _(dve):
            def step(k, u):
                t = k * SLOTS + u
                r = v.rows_of(t)
                dve.wait_ge(x2_loaded[u], 16 * (k + 1))
                dve.wait_ge(fetched[u], 16 * TOP * (k + 1))

                def w(i):
                    return v.weight[0:r, bass.ds(t, 1), i]

                nc.vector.scalar_tensor_tensor(out=one[u % 2][0:r, :], in0=got[u][0:r, 0, :], scalar=w(0),
                                               in1=x2[u][0:r, :], op0=ALU.mult, op1=ALU.add).then_inc(one_ready, 1)
                dve.wait_ge(one_ready, t + 1)
                if inside(k, t, SLOTS, NT):
                    dve.wait_ge(out_stored[u], 16 * k)
                nc.vector.scalar_tensor_tensor(out=final[u][0:r, :], in0=got[u][0:r, 1, :], scalar=w(1),
                                               in1=one[u % 2][0:r, :], op0=ALU.mult,
                                               op1=ALU.add).then_inc(final_ready, 1)

            run_steps(dve, SLOTS, NT, NT - 1, step)


_INS = ["x", "src", "dst", "L0_gnn_W1", "L0_gnn_b1", "L0_gnn_W2", "L0_gnn_b2", "L0_ffn_Wr", "L0_ffn_br",
        "L0_ffn_W1", "L0_ffn_b1", "L0_ffn_W2", "L0_ffn_b2"]


def kernel(**inputs):
    import numpy as _np
    import concourse.bacc as _bacc
    from concourse import mybir as _mybir
    from concourse.bass_utils import run_bass_kernel_spmd as _run

    nc = _bacc.Bacc("TRN2", target_bir_lowering=False, num_devices=1)
    arrays, args = {}, []
    for name in _INS:
        a = _np.ascontiguousarray(inputs[name])
        arrays[f"in_{name}_dram"] = a
        args.append(nc.dram_tensor(f"in_{name}_dram", a.shape, _mybir.dt.from_np(a.dtype), kind="ExternalInput").ap())
    shape = tuple(inputs["x"].shape)
    args.append(nc.dram_tensor("out_0_dram", shape, _mybir.dt.float32, kind="ExternalOutput").ap())
    gnn_moe_kernel(nc, *args)
    r = _run(nc, [arrays], core_ids=[0])
    return r.results[0]["out_0_dram"]
```

```python
from contextlib import ExitStack

import concourse.bass as bass
from concourse import mybir

F32 = mybir.dt.float32
F32R = mybir.dt.float32r
I32 = mybir.dt.int32
U32 = mybir.dt.uint32
ALU = mybir.AluOpType
ACT = mybir.ActivationFunctionType
AX_X = mybir.AxisListType.X

P = 128
EPS = 1e-5
TOP = 2
WIN = 96
GT = 4
ST = 4
NOWHERE = 1 << 20


def ceil_div(a, b):
    return -(-a // b)


def inside(k, t, low, high):
    return not isinstance(k, int) or low <= t < high


def run_steps(eng, slots, total, steady_end, body, peel=1):
    blocks = max(steady_end // slots, peel)
    for t in range(min(slots * peel, total)):
        body(t // slots, t % slots)
    if blocks > peel:
        with eng.Fori(peel, blocks) as k:
            for u in range(slots):
                body(k, u)
    for t in range(blocks * slots, total):
        body(t // slots, t % slots)


def back(k, u, d, slots):
    kk, uu = k + (u - d) // slots, (u - d) % slots
    return kk, uu, kk * slots + uu


def stand_for(eng, sem):
    eng.sem_inc(sem, 1)


class Chain:

    def __init__(self, eng, sem, base):
        self.eng, self.sem, self.base, self.n = eng, sem, base, 0

    def link(self, instruction):
        instruction.then_inc(self.sem, 1)
        self.n += 1
        self.eng.wait_ge(self.sem, self.base + self.n)


class Shared:
    pass


def gnn_moe_kernel(nc, x, src, dst, W1, b1, W2, b2, Wr, br, EW1, Eb1, EW2, Eb2, out):
    v = Shared()
    v.x, v.src, v.dst, v.out = x, src, dst, out
    v.W1, v.b1, v.W2, v.b2, v.Wr, v.br = W1, b1, W2, b2, Wr, br
    v.EW1, v.Eb1, v.EW2, v.Eb2 = EW1, Eb1, EW2, Eb2

    v.N, v.D = N, D = x.shape
    v.E = E = src.shape[0]
    v.NX, _, v.F = NX, _, F = EW1.shape
    v.C, v.FC = C, FC = D // P, F // P
    v.NT = NT = ceil_div(N, P)
    v.TAIL = TAIL = N - (NT - 1) * P
    v.NS = NS = ceil_div(NT, ST)
    v.SUP = SUP = ST * P
    v.NC = NC = NT * P + WIN
    v.ROUNDS = ROUNDS = ceil_div(N, WIN)
    v.GE = GE = GT * P
    v.NG = NG = ceil_div(E, GE)
    v.GB = GB = ceil_div(NG, P)
    assert D == 512 and F % P == 0 and NX == 8 and GB == 2 and ROUNDS * WIN <= NC
    assert NT % ST == 1 and NT > 2 * ST

    v.REGION = REGION = ceil_div(N + P, P) * P
    v.STEPS = STEPS = (TOP * N + NX * (P - 1)) // P

    v.normed = nc.dram_tensor("normed_rows", (N, D), F32, kind="Internal").ap()
    v.resid = nc.dram_tensor("residual_rows", (N, D), F32, kind="Internal").ap()
    v.sent = nc.dram_tensor("expert_in_rows", (NX * REGION, D), F32, kind="Internal").ap()
    v.made = nc.dram_tensor("expert_out_rows", (STEPS * P, D), F32, kind="Internal").ap()

    v.rows_of = lambda t: TAIL if isinstance(t, int) and t == NT - 1 else P
    v.tiles_of = lambda s: NT - (NS - 1) * ST if isinstance(s, int) and s == NS - 1 else ST
    v.width_of = lambda s: TAIL if isinstance(s, int) and s == NS - 1 else SUP

    with ExitStack() as whole:
        v.sem = sem = lambda name: whole.enter_context(nc.semaphore(name))
        v.sb = sb = lambda name, shape, dt=F32, ctx=whole: ctx.enter_context(nc.sbuf_tensor(name, shape, dt))
        v.ps = ps = lambda name, shape, dt=F32, ctx=whole: ctx.enter_context(nc.psum_tensor(name, shape, dt))

        v.ident = sb("ident", [P, P])
        v.ones = sb("ones", [P, P])
        v.before = sb("before", [P, P])
        v.eps = sb("eps", [P, 1])
        v.iota8 = sb("iota8", [P, ST, NX])
        v.region_row = sb("region_row", [P, NX])
        v.run_row = sb("run_row", [P, NX])
        v.place = sb("place", [P, NS * ST, TOP])
        v.weight = sb("weight", [P, NS * ST, TOP])

        v.const_ready = sem("const_ready")
        v.mlp_w_in = sem("mlp_w_in")
        v.mlp_w_ready = sem("mlp_w_ready")
        v.sp_waits_passed = sem("sp_waits_passed")
        v.waits_passed = sem("waits_passed")
        v.dve_waits_passed = sem("dve_waits_passed")

        with ExitStack() as nodes:
            v.node_cols = sb("node_cols", [P, C, NC], ctx=nodes)
            v.w1 = [sb(f"w1_{h}", [P, C, D], F32R, ctx=nodes) for h in range(2)]
            v.w2 = [sb(f"w2_{h}", [P, C, D], F32R, ctx=nodes) for h in range(2)]
            v.b1_col = sb("b1_col", [P, C], ctx=nodes)
            v.b2_all = sb("b2_all", [P, D], ctx=nodes)
            v.wr_sb = sb("wr_sb", [P, C, NX], ctx=nodes)
            v.br_all = sb("br_all", [P, ST, NX], ctx=nodes)

            with ExitStack() as edges:
                v.src_t = sb("src_t", [P, GB * P, GT], ctx=edges)
                v.dst_t = sb("dst_t", [P, GB * P, GT], ctx=edges)
                v.low_all = sb("low_all", [P, GB * P], ctx=edges)
                v.low_row = sb("low_row", [1, 2, GB * P], ctx=edges)
                v.low_int = sb("low_int", [1, GB * P], I32, ctx=edges)
                v.wide = sb("wide", [1, 2], ctx=edges)
                v.wide_int = sb("wide_int", [1, 1], I32, ctx=edges)
                v.starts = sb("starts", [P, ROUNDS], ctx=edges)
                v.iota_ps = ps("iota_ps", [P, 512], ctx=edges)

                normalize(nc, v)
                aggregate(nc, v)
            mlp_route(nc, v)
        experts(nc, v)
        combine(nc, v)


def normalize(nc, v):
    N, D, C, NT, NC, GB, E, GE = v.N, v.D, v.C, v.NT, v.NC, v.GB, v.E, v.GE
    sem = v.sem
    SLOTS = 8
    LAG = 2
    full, rest = divmod(E, GE)

    with ExitStack() as ctx:
        def sb(name, shape, dt=F32):
            return v.sb(name, shape, dt, ctx=ctx)

        def ps(name, shape, dt=F32):
            return v.ps(name, shape, dt, ctx=ctx)

        x_in = [sb(f"x_in{i}", [P, D]) for i in range(SLOTS)]
        x_norm = [sb(f"x_norm{i}", [P, D]) for i in range(SLOTS)]
        stats = sb("stats", [P, SLOTS, 6])
        meanvar = sb("meanvar", [P, SLOTS, 2])
        std = sb("std", [P, SLOTS])
        rstd = sb("rstd", [P, SLOTS])
        src_raw = sb("src_raw", [P, GB, GE], I32)
        dst_raw = sb("dst_raw", [P, GB, GE], I32)
        src_f = sb("src_f", [P, GB, GE])
        dst_f = sb("dst_f", [P, GB, GE])
        dst_real = sb("dst_real", [P, GB, GE])
        low = sb("low", [P, GB])
        high = sb("high", [P, GB])
        span = sb("span", [P, GB])
        iota_i = sb("iota_i", [P, WIN], I32)
        start_i = sb("start_i", [P, v.ROUNDS], I32)
        eight_i = sb("eight_i", [P, ST, v.NX], I32)
        region_i = sb("region_i", [P, v.NX], I32)
        turn = [ps(f"turn{i}", [P, C, P]) for i in range(2)]
        turn_edge = [ps(f"turn_edge{i}", [P, GT, P]) for i in range(2)]
        row_ps = ps("row_ps", [P, 2, GB * P])
        low_ps = ps("low_ps", [P, GB * P])

        pads_set = sem("pads_set")
        iotas_made = sem("iotas_made")
        tri_steps = sem("tri_steps")
        edges_in = sem("edges_in")
        edge_chain = sem("edge_chain")
        edges_float = sem("edges_float")
        edge_turned = sem("edge_turned")
        edge_copied = sem("edge_copied")
        rows_turned = sem("rows_turned")
        rows_copied = sem("rows_copied")
        low_spread = sem("low_spread")
        x_loaded = [sem(f"x_loaded{i}") for i in range(SLOTS)]
        x_stored = [sem(f"x_stored{i}") for i in range(SLOTS)]
        norm_chain = sem("norm_chain")
        var_ready = sem("var_ready")
        std_ready = sem("std_ready")
        norm_ready = sem("norm_ready")
        norm_turned = sem("norm_turned")
        cols_copied = sem("cols_copied")

        block = ctx.enter_context(nc.Block())

        @block.sync
        def _(sp):
            def load_x(k, u):
                t = k * SLOTS + u
                r = v.rows_of(t)
                sp.dma_start(x_in[u][0:r, :], v.x[bass.ds(t * P, r), :]).then_inc(x_loaded[u], 16)

            for t in range(SLOTS):
                load_x(0, t)
            sp.wait_ge(pads_set, 2)
            for raw, given in ((src_raw, v.src), (dst_raw, v.dst)):
                for b in range(GB):
                    n = min(full - b * P, P)
                    sp.dma_start(raw[0:n, b, :], given[b * P * GE:(b * P + n) * GE]
                                 .rearrange("(g e) -> g e", e=GE)).then_inc(edges_in, 16)
                if rest:
                    sp.dma_start(raw[full % P:full % P + 1, full // P, 0:rest],
                                 given[full * GE:E].rearrange("(g e) -> g e", g=1)).then_inc(edges_in, 16)

            def step(k, u):
                t = k * SLOTS + u
                r = v.rows_of(t)
                sp.wait_ge(norm_ready, t + 1)
                sp.dma_start(v.normed[bass.ds(t * P, r), :], x_norm[u][0:r, :]).then_inc(x_stored[u], 16)
                if inside(k, t + SLOTS, 0, NT):
                    load_x(k + 1, u)

            run_steps(sp, SLOTS, NT, NT - 1 - SLOTS, step)
            sp.dma_start(v.wr_sb[:, :, :], v.Wr.rearrange("(c p) n -> p c n", p=P)).then_inc(v.mlp_w_in, 16)
            sp.dma_start(v.b2_all[:, :], v.b2.partition_broadcast(P)).then_inc(v.mlp_w_in, 16)
            for j in range(ST):
                sp.dma_start(v.br_all[:, j, :], v.br.partition_broadcast(P)).then_inc(v.mlp_w_in, 16)
            sp.dma_start(v.b1_col[:, :], v.b1.rearrange("(c p) -> p c", p=P),
                         allow_slow_non_contiguous=True).then_inc(v.mlp_w_in, 16)
            for u in range(SLOTS):
                sp.wait_ge(x_stored[u], 16 * len(range(u, NT, SLOTS)))

        @block.gpsimd
        def _(pool):
            nc.gpsimd.memset(src_raw[:, :, :], 0).then_inc(pads_set, 1)
            nc.gpsimd.memset(dst_raw[:, :, :], NOWHERE).then_inc(pads_set, 1)
            nc.gpsimd.memset(v.ident[:, :], 0.0).then_inc(tri_steps, 1)
            nc.gpsimd.memset(v.before[:, :], 1.0).then_inc(tri_steps, 1)
            nc.gpsimd.memset(v.ones[:, :], 1.0).then_inc(v.const_ready, 1)
            nc.gpsimd.memset(v.eps[:, :], EPS).then_inc(v.const_ready, 1)
            nc.gpsimd.memset(v.node_cols[:, :, N:NC], 0.0).then_inc(v.const_ready, 1)
            pool.wait_ge(tri_steps, 2)
            nc.gpsimd.affine_select(out=v.ident[:, :], in_=v.ident[:, :], compare_op=ALU.not_equal, fill=1.0,
                                    base=0, pattern=[[-1, P]], channel_multiplier=1).then_inc(v.const_ready, 1)
            nc.gpsimd.affine_select(out=v.before[:, :], in_=v.before[:, :], compare_op=ALU.is_gt, fill=0.0,
                                    base=0, pattern=[[1, P]], channel_multiplier=-1).then_inc(v.const_ready, 1)
            nc.gpsimd.iota(iota_i[:, :], pattern=[[1, WIN]], base=0, channel_multiplier=0).then_inc(iotas_made, 1)
            nc.gpsimd.iota(start_i[:, :], pattern=[[WIN, v.ROUNDS]], base=0,
                           channel_multiplier=0).then_inc(iotas_made, 1)
            nc.gpsimd.iota(eight_i[:, :, :], pattern=[[0, ST], [1, v.NX]], base=0,
                           channel_multiplier=0).then_inc(iotas_made, 1)
            nc.gpsimd.iota(region_i[:, :], pattern=[[v.REGION, v.NX]], base=0,
                           channel_multiplier=0).then_inc(iotas_made, 1)

        @block.vector
        def _(dve):
            dve.wait_ge(iotas_made, 4)
            nc.vector.tensor_copy(v.iota_ps[:, 0:WIN], iota_i[:, :]).then_inc(v.const_ready, 1)
            nc.vector.tensor_copy(v.starts[:, :], start_i[:, :]).then_inc(v.const_ready, 1)
            nc.vector.tensor_copy(v.iota8[:, :, :], eight_i[:, :, :]).then_inc(v.const_ready, 1)
            nc.vector.tensor_copy(v.region_row[:, :], region_i[:, :]).then_inc(v.const_ready, 1)
            nc.vector.tensor_copy(v.run_row[:, :], region_i[:, :]).then_inc(v.const_ready, 1)

            def step(k, u):
                t = k * SLOTS + u
                if inside(k, t, 0, NT):
                    r = v.rows_of(t)
                    dve.wait_ge(x_loaded[u], 16 * (k + 1))
                    if inside(k, t, SLOTS, NT):
                        dve.wait_ge(std_ready, t - SLOTS + 1)
                    nc.vector.bn_stats(stats[0:r, u, :], x_in[u][0:r, :]).then_inc(norm_chain, 1)
                    dve.wait_ge(norm_chain, t + 1)
                    stand_for(dve, v.dve_waits_passed)
                    nc.vector.bn_aggr(meanvar[0:r, u, :], stats[0:r, u, :]).then_inc(var_ready, 1)
                kb, ub, tb = back(k, u, LAG, SLOTS)
                if inside(k, tb, 0, NT):
                    r = v.rows_of(tb)
                    dve.wait_ge(std_ready, tb + 1)
                    nc.vector.reciprocal(rstd[0:r, ub:ub + 1], std[0:r, ub:ub + 1]).then_inc(rstd_ready, 1)
                    dve.wait_ge(rstd_ready, tb + 1)
                    dve.wait_ge(var_ready, tb + 1)
                    if inside(k, tb, SLOTS, NT):
                        dve.wait_ge(x_stored[ub], 16 * kb)
                        dve.wait_ge(norm_turned, tb - SLOTS + 1)
                    nc.vector.tensor_scalar(x_norm[ub][0:r, :], x_in[ub][0:r, :], meanvar[0:r, ub, 0:1],
                                            rstd[0:r, ub:ub + 1], ALU.subtract, ALU.mult).then_inc(norm_ready, 1)

            rstd_ready = v.sem("rstd_ready")
            run_steps(dve, SLOTS, NT + LAG, NT - 1, step, peel=2)

            dve.wait_ge(edges_in, 16 * 2 * (GB + (rest > 0)))
            nc.vector.tensor_copy(src_f[:, :, :], src_raw[:, :, :]).then_inc(edges_float, 1)
            c = Chain(dve, edge_chain, 0)
            c.link(nc.vector.tensor_copy(dst_f[:, :, :], dst_raw[:, :, :]))
            nc.vector.tensor_reduce(low[:, :], dst_f[:, :, :], AX_X, ALU.min).then_inc(edges_float, 1)
            c.link(nc.vector.scalar_tensor_tensor(out=dst_real[:, :, :], in0=dst_f[:, :, :],
                                                  scalar=float(NOWHERE // 2), in1=dst_f[:, :, :],
                                                  op0=ALU.is_lt, op1=ALU.mult))
            c.link(nc.vector.tensor_reduce(high[:, :], dst_real[:, :, :], AX_X, ALU.max))
            dve.wait_ge(edges_float, 2)
            nc.vector.tensor_tensor(span[:, :], high[:, :], low[:, :], ALU.subtract).then_inc(edges_float, 1)
            for n, (table, b) in enumerate([(tab, b) for tab in (v.src_t, v.dst_t) for b in range(GB)]):
                dve.wait_ge(edge_turned, n + 1)
                nc.vector.tensor_copy(table[:, b * P:(b + 1) * P, :],
                                      turn_edge[n % 2][:, :, :].rearrange("p j g -> p g j")).then_inc(edge_copied, 1)
            dve.wait_ge(rows_turned, 1)
            c.link(nc.vector.tensor_copy(v.low_row[:, :, :], row_ps[0:1, :, :]))
            nc.vector.tensor_copy(v.low_int[:, :], v.low_row[:, 0, :]).then_inc(rows_copied, 1)
            c.link(nc.vector.tensor_reduce(v.wide[:, 0:1], v.low_row[:, 1, :], AX_X, ALU.max))
            nc.vector.tensor_scalar(v.wide_int[:, :], v.wide[:, 0:1], float(WIN), None,
                                    ALU.is_ge).then_inc(rows_copied, 1)
            dve.wait_ge(low_spread, 1)
            nc.vector.tensor_copy(v.low_all[:, :], low_ps[:, :]).then_inc(rows_copied, 1)

        @block.scalar
        def _(act):
            act.wait_ge(v.const_ready, 10)

            def step(k, u):
                t = k * SLOTS + u
                if inside(k, t, 0, NT):
                    r = v.rows_of(t)
                    act.wait_ge(var_ready, t + 1)
                    if inside(k, t, SLOTS, NT):
                        act.wait_ge(norm_ready, t - SLOTS + 1)
                    nc.scalar.activation(std[0:r, u:u + 1], meanvar[0:r, u, 1:2], ACT.Sqrt,
                                         bias=v.eps[0:r, :]).then_inc(std_ready, 1)
                kb, ub, tb = back(k, u, LAG + 1, SLOTS)
                if inside(k, tb, 0, NT):
                    r = v.rows_of(tb)
                    act.wait_ge(norm_turned, tb + 1)
                    nc.scalar.activation(v.node_cols[:, :, bass.ds(tb * P, r)], turn[ub % 2][:, :, 0:r],
                                         ACT.Copy).then_inc(cols_copied, 1)

            run_steps(act, SLOTS, NT + LAG + 1, NT - 1, step)

        @block.tensor
        def _(pe):
            pe.wait_ge(v.const_ready, 10)

            def step(k, u):
                t = k * SLOTS + u
                r = v.rows_of(t)
                pe.wait_ge(norm_ready, t + 1)
                if inside(k, t, 2, NT):
                    pe.wait_ge(cols_copied, t - 1)
                for c in range(C):
                    last = nc.tensor.transpose(turn[u % 2][:, c, 0:r], x_norm[u][0:r, c * P:(c + 1) * P],
                                               v.ident[0:r, 0:r])
                last.then_inc(norm_turned, 1)

            run_steps(pe, SLOTS, NT, NT - 1, step)
            pe.wait_ge(edges_float, 1)
            pe.wait_ge(edge_chain, 1)
            for n, (table, b) in enumerate([(tab, b) for tab in (src_f, dst_f) for b in range(GB)]):
                if n >= 2:
                    pe.wait_ge(edge_copied, n - 1)
                for j in range(GT):
                    last = nc.tensor.transpose(turn_edge[n % 2][:, j, :], table[:, b, j * P:(j + 1) * P],
                                               v.ident[:, :])
                last.then_inc(edge_turned, 1)
            pe.wait_ge(edges_float, 3)
            for n, col in enumerate((low, span)):
                for b in range(GB):
                    last = nc.tensor.transpose(row_ps[0:1, n, b * P:(b + 1) * P], col[:, b:b + 1], v.ident[:, :])
            last.then_inc(rows_turned, 1)
            pe.wait_ge(edge_chain, 4)
            nc.tensor.matmul(low_ps[:, :], v.ones[0:1, :], v.low_row[0:1, 0, :], start=True,
                             stop=True).then_inc(low_spread, 1)


def aggregate(nc, v):
    D, C, NG, ROUNDS, N = v.D, v.C, v.NG, v.ROUNDS, v.N
    sem = v.sem
    SLOTS = 4
    LAG = 1

    with ExitStack() as ctx:
        edge_rows = [v.sb(f"edge_rows{i}", [P, GT, D], ctx=ctx) for i in range(SLOTS)]
        index = [v.sb(f"index{i}", [P, GT], I32, ctx=ctx) for i in range(SLOTS)]
        hot = [v.sb(f"hot{i}", [P, GT, WIN], ctx=ctx) for i in range(2)]
        w_raw = [v.sb(f"w_raw{i}", [P, C, D], ctx=ctx) for i in range(2)]
        sums = [v.ps(f"sums{i}", [P, 512], ctx=ctx) for i in range(2)]

        w_in = sem("w_in")
        w_high_made = sem("w_high_made")
        index_ready = sem("index_ready")
        gathered = [sem(f"gathered{i}") for i in range(SLOTS)]
        hot_ready = sem("hot_ready")
        sums_ready = sem("sums_ready")
        added = sem("added")
        every_index_ready = sem("every_index_ready")
        every_gathered = sem("every_gathered")
        every_hot_ready = sem("every_hot_ready")
        every_sums_ready = sem("every_sums_ready")
        every_added = sem("every_added")

        def sums_of(i):
            return sums[i][:, 0:C * WIN].rearrange("p (c w) -> p c w", c=C)

        def is_wide(eng):
            return eng.value_load(v.wide_int[0:1, 0:1], min_val=0, max_val=1)

        def gather(u, signal):
            for j in range(GT):
                nc.gpsimd.indirect_dma_start(
                    out=edge_rows[u][:, j, :], out_offset=None, in_=v.normed[:, :],
                    in_offset=bass.IndirectOffsetOnAxis(ap=index[u][:, j:j + 1], axis=0)).then_inc(signal, 16)

        def one_hots(h, first, g, signal):
            for j in range(GT):
                last = nc.vector.tensor_scalar(hot[h][:, j, :], v.iota_ps[:, 0:WIN], first,
                                               v.dst_t[:, bass.ds(g, 1), j], ALU.add, ALU.is_equal)
            last.then_inc(signal, 1)

        def products(u, h, signal):
            for c in range(C):
                for j in range(GT):
                    last = nc.tensor.matmul(sums_of(h)[:, c, :], edge_rows[u][:, j, c * P:(c + 1) * P],
                                            hot[h][:, j, :], start=(j == 0), stop=(j == GT - 1))
            last.then_inc(signal, 1)

        def add_window(h, start, signal):
            window = v.node_cols[:, :, bass.ds(start, WIN)]
            nc.vector.tensor_tensor(window, sums_of(h), window, ALU.add).then_inc(signal, 1)

        def weights_high(act):
            act.wait_ge(w_in, 16 * 2)
            for i, w in enumerate((v.w1, v.w2)):
                nc.scalar.activation(w[0][:, :, :], w_raw[i][:, :, :], ACT.Copy).then_inc(w_high_made, 1)

        def weight_low(dve, i, w):
            dve.wait_ge(w_high_made, i + 1)
            nc.vector.tensor_tensor(w[1][:, :, :], w_raw[i][:, :, :], w[0][:, :, :].bitcast(F32),
                                    ALU.subtract).then_inc(v.mlp_w_ready, 1)

        block = ctx.enter_context(nc.Block())

        @block.sync
        def _(sp):
            for raw, given in zip(w_raw, (v.W1, v.W2)):
                sp.dma_start(raw[:, :, :], given.rearrange("(c p) n -> p c n", p=P)).then_inc(w_in, 16)

        @block.scalar
        def _(act):
            def step(k, u):
                t = k * SLOTS + u
                if inside(k, t, SLOTS, NG):
                    act.wait_ge(gathered[u], 16 * GT * k)
                nc.scalar.activation(index[u][:, :], v.src_t[:, bass.ds(t, 1), :].rearrange("p g j -> p (g j)"),
                                     ACT.Copy).then_inc(index_ready, 1)
                if not inside(k, t, SLOTS, NG) and u == SLOTS - 1:
                    weights_high(act)

            def every(g, first):
                if not first:
                    act.wait_ge(every_gathered, 16 * GT * g)
                nc.scalar.activation(index[0][:, :], v.src_t[:, bass.ds(g, 1), :].rearrange("p g j -> p (g j)"),
                                     ACT.Copy).then_inc(every_index_ready, 1)

            wide = is_wide(act)
            with act.If(wide == 0):
                run_steps(act, SLOTS, NG, NG, step)
            with act.Else():
                weights_high(act)
                every(0, True)
                with act.Fori(1, NG) as g:
                    every(g, False)

        @block.gpsimd
        def _(pool):
            def step(k, u):
                t = k * SLOTS + u
                pool.wait_ge(index_ready, t + 1)
                if inside(k, t, SLOTS, NG):
                    pool.wait_ge(sums_ready, t - SLOTS + 1)
                stand_for(pool, v.waits_passed)
                gather(u, gathered[u])

            def every(g, first):
                pool.wait_ge(every_index_ready, g + 1)
                if not first:
                    pool.wait_ge(every_sums_ready, g * ROUNDS)
                stand_for(pool, v.waits_passed)
                gather(0, every_gathered)

            wide = is_wide(pool)
            with pool.If(wide == 0):
                run_steps(pool, SLOTS, NG, NG, step)
            with pool.Else():
                every(0, True)
                with pool.Fori(1, NG) as g:
                    every(g, False)

        @block.vector
        def _(dve):
            def step(k, u):
                t = k * SLOTS + u
                if inside(k, t, 0, NG):
                    if inside(k, t, 2, NG):
                        dve.wait_ge(sums_ready, t - 1)
                    one_hots(u % 2, v.low_all[:, bass.ds(t, 1)], t, hot_ready)
                kb, ub, tb = back(k, u, LAG, SLOTS)
                if inside(k, tb, 0, NG):
                    start = dve.value_load(v.low_int[0:1, bass.ds(tb, 1)], min_val=0, max_val=N - 1)
                    dve.wait_ge(sums_ready, tb + 1)
                    if inside(k, tb, 1, NG):
                        dve.wait_ge(added, tb)
                    add_window(ub % 2, start, added)
                if not inside(k, t, SLOTS, NG) and u >= SLOTS - 2:
                    weight_low(dve, u - (SLOTS - 2), (v.w1, v.w2)[u - (SLOTS - 2)])

            def every(g, first):
                def window(r, first_window):
                    n = g * ROUNDS + r
                    one_hots(0, v.starts[:, bass.ds(r, 1)], g, every_hot_ready)
                    dve.wait_ge(every_sums_ready, n + 1)
                    if not first_window:
                        dve.wait_ge(every_added, n)
                    add_window(0, r * WIN, every_added)

                window(0, first)
                with dve.Fori(1, ROUNDS) as r:
                    window(r, False)

            wide = is_wide(dve)
            with dve.If(wide == 0):
                run_steps(dve, SLOTS, NG + LAG, NG, step)
            with dve.Else():
                weight_low(dve, 0, v.w1)
                weight_low(dve, 1, v.w2)
                every(0, True)
                with dve.Fori(1, NG) as g:
                    every(g, False)

        @block.tensor
        def _(pe):
            def step(k, u):
                t = k * SLOTS + u
                pe.wait_ge(gathered[u], 16 * GT * (k + 1))
                pe.wait_ge(hot_ready, t + 1)
                if inside(k, t, 2, NG):
                    pe.wait_ge(added, t - 1)
                products(u, u % 2, sums_ready)

            def every(g):
                with pe.Fori(0, ROUNDS) as r:
                    pe.wait_ge(every_gathered, 16 * GT * (g + 1))
                    pe.wait_ge(every_hot_ready, g * ROUNDS + r + 1)
                    products(0, 0, every_sums_ready)

            wide = is_wide(pe)
            with pe.If(wide == 0):
                run_steps(pe, SLOTS, NG, NG, step)
            with pe.Else():
                with pe.Fori(0, NG) as g:
                    every(g)


def mlp_route(nc, v):
    N, D, C, NX, NT, NS, SUP = v.N, v.D, v.C, v.NX, v.NT, v.NS, v.SUP
    sem, tiles_of, width_of = v.sem, v.tiles_of, v.width_of
    SLOTS = 2

    with ExitStack() as ctx:
        def sb(name, shape, dt=F32):
            return v.sb(name, shape, dt, ctx=ctx)

        def ps(name, shape, dt=F32):
            return v.ps(name, shape, dt, ctx=ctx)

        x2 = [sb(f"x2_{i}", [P, ST, D]) for i in range(SLOTS)]
        xn = [sb(f"xn_{i}", [P, ST, D]) for i in range(SLOTS)]
        xn_col = sb("xn_col", [P, C, P])
        cols = [sb(f"cols_{h}", [P, C, SUP], F32R) for h in range(2)]
        hidden = [sb(f"hidden_{h}", [P, C, SUP], F32R) for h in range(2)]
        full = sb("full", [P, SUP])
        stats = sb("stats2", [P, ST, 6])
        meanvar = sb("meanvar2", [P, ST, 2])
        std = sb("std2", [P, ST])
        rstd = sb("rstd2", [P, ST])
        logit = sb("logit", [P, ST, NX])
        peak = sb("peak", [P, ST])
        shifted = sb("shifted", [P, ST, NX])
        expd = sb("expd", [P, ST, NX])
        total = sb("total", [P, ST])
        inverse = sb("inverse", [P, ST])
        prob = sb("prob", [P, ST, NX])
        best = sb("best", [P, ST, NX])
        chosen = sb("chosen", [P, ST, NX], U32)
        chosen_f = sb("chosen_f", [P, ST, NX])
        pick = [sb(f"pick{i}", [P, ST, NX]) for i in range(TOP)]
        picked = sb("picked", [P, ST, NX])
        row_of = sb("row_of", [P, ST, NX])
        row_pick = [sb(f"row_pick{i}", [P, ST, NX]) for i in range(TOP)]
        row_now = sb("row_now", [P, ST, TOP])
        row_int = [sb(f"row_int{i}", [P, TOP, ST], I32) for i in range(SLOTS)]

        hid_ps = [ps(f"hid_ps{i}", [P, SUP]) for i in range(2)]
        out_ps = [ps(f"out_ps{i}", [P, D]) for i in range(2)]
        turn = [ps(f"turn2_{i}", [P, C, P]) for i in range(2)]
        logit_ps = ps("logit_ps", [P, ST, NX])
        rank_ps = ps("rank_ps", [P, 2, ST, NX])

        x_loaded = [sem(f"xr_loaded{i}") for i in range(SLOTS)]
        x2_stored = [sem(f"x2_stored{i}") for i in range(SLOTS)]
        scattered = [sem(f"scattered{i}") for i in range(SLOTS)]
        hid_made = sem("hid_made")
        hid_copied = sem("hid_copied")
        hid_low_ready = sem("hid_low_ready")
        node_high_ready = sem("node_high_ready")
        node_low_ready = sem("node_low_ready")
        out_made = sem("out_made")
        out_copied = sem("out_copied")
        epi_chain = sem("epi_chain")
        var_ready = sem("var_ready2")
        std_ready = sem("std_ready2")
        rstd_ready = sem("rstd_ready2")
        xn_ready = sem("xn_ready")
        xn_turned = sem("xn_turned")
        xn_copied = sem("xn_copied")
        xn_col_used = sem("xn_col_used")
        shifted_ready = sem("shifted_ready")
        exp_ready = sem("exp_ready")
        route_chain = sem("route_chain")
        picked_ready = sem("picked_ready")
        ranks_ready = sem("ranks_ready")
        place_chain = sem("place_chain")
        place_ready = sem("place_ready")

        def shape_of(s):
            n = tiles_of(s)
            return n, (v.TAIL if n == 1 else P)

        PASSES = [(c, a, b) for c in range(C) for a, b in ((0, 0), (0, 1), (1, 0))]

        STEPS = NS + 2
        STEADY = NS - 2

        block = ctx.enter_context(nc.Block())

        @block.sync
        def _(sp):
            def rows(dram, s):
                n, r = shape_of(s)
                return dram[bass.ds(s * SUP, width_of(s)), :].rearrange("(j p) d -> p j d", p=r)

            def load(k, u, s):
                n, r = shape_of(s)
                sp.dma_start(x2[u][0:r, 0:n, :], rows(v.x, s)).then_inc(x_loaded[u], 16)

            load(0, 0, 0)
            load(0, 1, 1)

            def step(k, u):
                s = k * SLOTS + u
                n, r = shape_of(s)
                sp.wait_ge(var_ready, s * ST + n)
                sp.dma_start(rows(v.resid, s), x2[u][0:r, 0:n, :]).then_inc(x2_stored[u], 16)
                if inside(k, s + SLOTS, 0, NS):
                    sp.wait_ge(x2_stored[u], 16 * (k + 1))
                    stand_for(sp, v.sp_waits_passed)
                    sp.wait_ge(xn_ready, (s + 1) * ST)
                    nxt = s + SLOTS
                    load(k + 1, u, nxt)

            run_steps(sp, SLOTS, NS, NS - 1 - SLOTS, step)
            for u in range(SLOTS):
                sp.wait_ge(x2_stored[u], 16 * len(range(u, NS, SLOTS)))

        @block.tensor
        def _(pe):
            pe.wait_ge(v.mlp_w_in, 16 * 7)
            pe.wait_ge(v.mlp_w_ready, 2)

            def first_layer(s):
                w = width_of(s)
                for m in range(C):
                    n = s * C + m
                    if inside(s, n, 2, NS * C):
                        pe.wait_ge(hid_copied, n - 1)
                    if m == 0:
                        pe.wait_ge(node_low_ready, s + 1)
                    for i, (c, a, b) in enumerate(PASSES):
                        last = nc.tensor.matmul(hid_ps[m % 2][:, 0:w], v.w1[a][:, c, m * P:(m + 1) * P],
                                                cols[b][:, c, 0:w], start=(i == 0), stop=(i == len(PASSES) - 1))
                    last.then_inc(hid_made, 1)

            def second_layer(s, j):
                _, r = shape_of(s)
                n = s * ST + j
                if j == 0:
                    pe.wait_ge(hid_low_ready, (s + 1) * C)
                if inside(s, n, 2, NT):
                    pe.wait_ge(out_copied, n - 1)
                for i, (c, a, b) in enumerate(PASSES):
                    last = nc.tensor.matmul(out_ps[j % 2][0:r, :], hidden[a][:, c, j * P:j * P + r],
                                            v.w2[b][:, c, :], start=(i == 0), stop=(i == len(PASSES) - 1))
                last.then_inc(out_made, 1)

            def turn_rows(s, u, j):
                _, r = shape_of(s)
                n = s * ST + j
                pe.wait_ge(xn_ready, n + 1)
                if inside(s, n, 2, NT):
                    pe.wait_ge(xn_copied, n - 1)
                for c in range(C):
                    last = nc.tensor.transpose(turn[j % 2][:, c, 0:r], xn[u][0:r, j, c * P:(c + 1) * P],
                                               v.ident[0:r, 0:r])
                last.then_inc(xn_turned, 1)

            def logits(s, j):
                _, r = shape_of(s)
                n = s * ST + j
                pe.wait_ge(xn_copied, n + 1)
                if j == 0 and inside(s, n, ST, NT):
                    pe.wait_ge(shifted_ready, s)
                for c in range(C):
                    last = nc.tensor.matmul(logit_ps[0:r, j, :], xn_col[:, c, 0:r], v.wr_sb[:, c, :],
                                            start=(c == 0), stop=(c == C - 1))
                last.then_inc(xn_col_used, 1)

            def ranks(s):
                n, r = shape_of(s)
                pe.wait_ge(picked_ready, s + 1)
                if inside(s, s, 1, NS):
                    pe.wait_ge(place_ready, s)
                mask = picked[0:r, 0:n, :]
                nc.tensor.matmul(rank_ps[0:r, 0, 0:n, :], v.before[0:r, 0:r], mask, start=True, stop=True)
                nc.tensor.matmul(rank_ps[:, 1, 0:n, :], v.ones[0:r, :], mask, start=True,
                                 stop=True).then_inc(ranks_ready, 1)

            def step(k, u):
                s = k * SLOTS + u
                _, ub, sb_ = back(k, u, 1, SLOTS)
                now, last = inside(k, s, 0, NS), inside(k, sb_, 0, NS)
                if now:
                    first_layer(s)
                if inside(k, s - 2, 0, NS):
                    ranks(s - 2)
                if last:
                    turn_rows(sb_, ub, 0)
                for j in range(ST):
                    if last and j + 1 < tiles_of(sb_):
                        turn_rows(sb_, ub, j + 1)
                    if last and j < tiles_of(sb_):
                        logits(sb_, j)
                    if now and j < tiles_of(s):
                        second_layer(s, j)

            run_steps(pe, SLOTS, STEPS, STEADY, step, peel=2)

        @block.scalar
        def _(act):
            act.wait_ge(v.mlp_w_in, 16 * 7)

            def high_part(s):
                w = width_of(s)
                if not isinstance(s, int) or s >= 1:
                    act.wait_ge(hid_made, s * C)
                nc.scalar.activation(cols[0][:, :, 0:w], v.node_cols[:, :, bass.ds(s * SUP, w)],
                                     ACT.Copy).then_inc(node_high_ready, 1)

            def hidden_high(s, m):
                w = width_of(s)
                act.wait_ge(hid_made, s * C + m + 1)
                if m == 0 and (not isinstance(s, int) or s >= 1):
                    act.wait_ge(out_made, s * ST)
                    act.wait_ge(var_ready, s * ST)
                if m > 0:
                    act.wait_ge(hid_low_ready, s * C + m)
                nc.scalar.activation(full[:, 0:w], hid_ps[m % 2][:, 0:w], ACT.Relu, bias=v.b1_col[:, m:m + 1])
                nc.scalar.activation(hidden[0][:, m, 0:w], hid_ps[m % 2][:, 0:w], ACT.Relu,
                                     bias=v.b1_col[:, m:m + 1]).then_inc(hid_copied, 1)

            high_part(0)
            hidden_high(0, 0)

            def step(k, u):
                s = k * SLOTS + u
                _, ub, sl = back(k, u, 1, SLOTS)
                if inside(k, s, 0, NS):
                    for m in range(1, C):
                        hidden_high(s, m)
                following = inside(k, s, 0, NS) and inside(k, s + 1, 0, NS)
                if following and not inside(k, sl, 0, NS):
                    high_part(s + 1)
                if inside(k, sl, 0, NS):
                    n, r = shape_of(sl)
                    for j in range(n):
                        if following and j == 1:
                            high_part(s + 1)
                        t = sl * ST + j
                        act.wait_ge(xn_turned, t + 1)
                        if inside(k, t, 1, NT):
                            act.wait_ge(xn_col_used, t)
                        nc.scalar.activation(xn_col[:, :, 0:r], turn[j % 2][:, :, 0:r],
                                             ACT.Copy).then_inc(xn_copied, 1)
                    act.wait_ge(shifted_ready, sl + 1)
                    nc.scalar.activation(expd[0:r, 0:n, :], shifted[0:r, 0:n, :], ACT.Exp).then_inc(exp_ready, 1)
                if following:
                    hidden_high(s + 1, 0)
                if inside(k, s, 0, NS):
                    n, r = shape_of(s)
                    act.wait_ge(var_ready, s * ST + n)
                    if inside(k, s, 1, NS):
                        act.wait_ge(rstd_ready, s)
                    nc.scalar.activation(std[0:r, 0:n], meanvar[0:r, 0:n, 1], ACT.Sqrt,
                                         bias=v.eps[0:r, :]).then_inc(std_ready, 1)

            run_steps(act, SLOTS, NS + 1, STEADY, step)

        @block.vector
        def _(dve):
            dve.wait_ge(v.mlp_w_in, 16 * 7)
            EPI = 2 * ST
            ROUTE = 9
            PLACE = 2 * ST + 2

            def low_part(s):
                w = width_of(s)
                dve.wait_ge(node_high_ready, s + 1)
                nc.vector.tensor_tensor(cols[1][:, :, 0:w], v.node_cols[:, :, bass.ds(s * SUP, w)],
                                        cols[0][:, :, 0:w].bitcast(F32), ALU.subtract).then_inc(node_low_ready, 1)

            def hidden_low(s, chunks):
                w = width_of(s)
                for m in chunks:
                    dve.wait_ge(hid_copied, s * C + m + 1)
                    nc.vector.tensor_tensor(hidden[1][:, m, 0:w], full[:, 0:w],
                                            hidden[0][:, m, 0:w].bitcast(F32), ALU.subtract).then_inc(hid_low_ready, 1)

            low_part(0)
            hidden_low(0, [0])

            def residual(k, u, s):
                n, r = shape_of(s)
                c = Chain(dve, epi_chain, s * EPI)
                dve.wait_ge(x_loaded[u], 16 * (k + 1))
                dve.wait_ge(hid_low_ready, (s + 1) * C)
                if inside(k, s, 1, NS):
                    dve.wait_ge(std_ready, s)
                    dve.wait_ge(xn_ready, s * ST)
                for j in range(n):
                    dve.wait_ge(out_made, s * ST + j + 1)
                    rows = x2[u][0:r, j, :]
                    add = nc.vector.tensor_tensor(full[0:r, :], out_ps[j % 2][0:r, :], v.b2_all[0:r, :], ALU.add)
                    add.then_inc(out_copied, 1)
                    dve.wait_ge(out_copied, s * ST + j + 1)
                    ins = nc.vector.scalar_tensor_tensor(out=rows, in0=full[0:r, :], scalar=0.0, in1=rows,
                                                         op0=ALU.max, op1=ALU.add)
                    c.link(ins)
                    c.link(nc.vector.bn_stats(stats[0:r, j, :], rows))
                    if j == 1 and inside(k, s + 1, 0, NS):
                        low_part(s + 1)
                stand_for(dve, v.dve_waits_passed)
                for j in range(n):
                    nc.vector.bn_aggr(meanvar[0:r, j, :], stats[0:r, j, :]).then_inc(var_ready, 1)

            def route(k, s):
                n, r = shape_of(s)
                c = Chain(dve, route_chain, s * ROUTE)

                def wide(t):
                    return t[0:r, 0:n].unsqueeze(2).to_broadcast([r, n, NX])

                dve.wait_ge(xn_col_used, s * ST + n)
                c.link(nc.vector.tensor_tensor(logit[0:r, 0:n, :], logit_ps[0:r, 0:n, :], v.br_all[0:r, 0:n, :],
                                               ALU.add))
                c.link(nc.vector.tensor_reduce(peak[0:r, 0:n], logit[0:r, 0:n, :], AX_X, ALU.max))
                if inside(k, s, 1, NS):
                    dve.wait_ge(exp_ready, s)
                nc.vector.tensor_tensor(shifted[0:r, 0:n, :], logit[0:r, 0:n, :], wide(peak),
                                        ALU.subtract).then_inc(shifted_ready, 1)
                dve.wait_ge(exp_ready, s + 1)
                c.link(nc.vector.tensor_reduce(total[0:r, 0:n], expd[0:r, 0:n, :], AX_X, ALU.add))
                c.link(nc.vector.reciprocal(inverse[0:r, 0:n], total[0:r, 0:n]))
                c.link(nc.vector.tensor_tensor(prob[0:r, 0:n, :], expd[0:r, 0:n, :], wide(inverse), ALU.mult))
                stand_for(dve, v.dve_waits_passed)
                for j in range(n):
                    nc.vector.max(best[0:r, j, :], prob[0:r, j, :]).then_inc(best_ready, 1)
                dve.wait_ge(best_ready, s * ST + n)
                stand_for(dve, v.dve_waits_passed)
                for j in range(n):
                    nc.vector.max_index(chosen[0:r, j, :], best[0:r, j, :],
                                        prob[0:r, j, :]).then_inc(chosen_ready, 1)
                dve.wait_ge(chosen_ready, s * ST + n)
                c.link(nc.vector.tensor_copy(v.weight[0:r, bass.ds(s * ST, n), :], best[0:r, 0:n, 0:TOP]))
                c.link(nc.vector.tensor_copy(chosen_f[0:r, 0:n, :], chosen[0:r, 0:n, :]))
                for i in range(TOP):
                    c.link(nc.vector.tensor_tensor(
                        pick[i][0:r, 0:n, :], v.iota8[0:r, 0:n, :],
                        chosen_f[0:r, 0:n, i].unsqueeze(2).to_broadcast([r, n, NX]), ALU.is_equal))
                nc.vector.tensor_tensor(picked[0:r, 0:n, :], pick[0][0:r, 0:n, :], pick[1][0:r, 0:n, :],
                                        ALU.add).then_inc(picked_ready, 1)
                assert c.n == ROUTE

            def norm(k, u, s):
                n, r = shape_of(s)
                dve.wait_ge(std_ready, s + 1)
                nc.vector.reciprocal(rstd[0:r, 0:n], std[0:r, 0:n]).then_inc(rstd_ready, 1)
                dve.wait_ge(rstd_ready, s + 1)
                if inside(k, s, SLOTS, NS):
                    dve.wait_ge(scattered[u], 16 * TOP * ST * k)
                for j in range(n):
                    nc.vector.tensor_scalar(xn[u][0:r, j, :], x2[u][0:r, j, :], meanvar[0:r, j, 0:1],
                                            rstd[0:r, j:j + 1], ALU.subtract, ALU.mult).then_inc(xn_ready, 1)

            def rows_for(k, u, s):
                n, r = shape_of(s)
                c = Chain(dve, place_chain, s * PLACE)
                dve.wait_ge(ranks_ready, s + 1)
                for j in range(n):
                    c.link(nc.vector.tensor_tensor(row_of[0:r, j, :], rank_ps[0:r, 0, j, :], v.run_row[0:r, :],
                                                   ALU.add))
                    c.link(nc.vector.tensor_tensor(v.run_row[:, :], rank_ps[:, 1, j, :], v.run_row[:, :], ALU.add))
                if inside(k, s, SLOTS, NS):
                    dve.wait_ge(scattered[u], 16 * TOP * ST * k)
                for i in range(TOP):
                    nc.vector.tensor_tensor(row_pick[i][0:r, 0:n, :], pick[i][0:r, 0:n, :], row_of[0:r, 0:n, :],
                                            ALU.mult).then_inc(pick_mult, 1)
                dve.wait_ge(pick_mult, TOP * (s + 1))
                for i in range(TOP):
                    c.link(nc.vector.tensor_reduce(row_now[0:r, 0:n, i], row_pick[i][0:r, 0:n, :], AX_X, ALU.add))
                nc.vector.tensor_copy(v.place[0:r, bass.ds(s * ST, n), :],
                                      row_now[0:r, 0:n, :]).then_inc(place_kept, 1)
                nc.vector.tensor_copy(row_int[u][0:r, :, 0:n],
                                      row_now[0:r, 0:n, :].rearrange("p j i -> p i j")).then_inc(place_ready, 1)
                dve.wait_ge(place_ready, s + 1)

            def step(k, u):
                s = k * SLOTS + u
                kb, ub, sl = back(k, u, 1, SLOTS)
                now, last = inside(k, s, 0, NS), inside(k, sl, 0, NS)
                if now:
                    hidden_low(s, range(1, C))
                if inside(k, s - 2, 0, NS):
                    rows_for(k - 1, u, s - 2)
                if now:
                    residual(k, u, s)
                if last:
                    route(kb, sl)
                if now and inside(k, s + 1, 0, NS):
                    hidden_low(s + 1, [0])
                if now:
                    norm(k, u, s)

            pick_mult = v.sem("pick_mult")
            best_ready = v.sem("best_ready")
            chosen_ready = v.sem("chosen_ready")
            place_kept = v.sem("place_kept")
            run_steps(dve, SLOTS, STEPS, STEADY, step, peel=2)

        @block.gpsimd
        def _(pool):
            def step(k, u):
                s = k * SLOTS + u
                n, r = shape_of(s)
                pool.wait_ge(place_ready, s + 1)
                pool.wait_ge(xn_ready, s * ST + n)
                stand_for(pool, v.waits_passed)
                for j in range(n):
                    for i in range(TOP):
                        nc.gpsimd.indirect_dma_start(
                            out=v.sent[:, :],
                            out_offset=bass.IndirectOffsetOnAxis(ap=row_int[u][0:r, i, j:j + 1], axis=0),
                            in_=xn[u][0:r, j, :], in_offset=None).then_inc(scattered[u], 16)

            run_steps(pool, SLOTS, NS, NS - 1, step)
            for u in range(SLOTS):
                pool.wait_ge(scattered[u], 16 * TOP * sum(tiles_of(s) for s in range(u, NS, SLOTS)))


def experts(nc, v):
    N, D, F, FC, C, NX, STEPS, REGION = v.N, v.D, v.F, v.FC, v.C, v.NX, v.STEPS, v.REGION
    sem = v.sem
    SLOTS = 8
    RING = 4

    def turn(k, u):
        return k * (SLOTS // RING) + u // RING


    with ExitStack() as ctx:
        def sb(name, shape, dt=F32):
            return v.sb(name, shape, dt, ctx=ctx)

        w1 = [sb(f"expert_w1_{i}", [P, NX * C * F], F32R) for i in range(2)]
        w2 = [sb(f"expert_w2_{i}", [P, NX * FC * D], F32R) for i in range(2)]
        w1_raw = sb("expert_w1_raw", [P, C * F])
        w2_raw = sb("expert_w2_raw", [P, FC * D])
        bias1 = sb("expert_b1", [P, NX * F])
        bias2 = sb("expert_b2", [P, NX * D])
        zeros = sb("zeros", [P, D])
        rows_in = [sb(f"rows_in{i}", [P, D]) for i in range(RING)]
        cols_in = [[sb(f"cols_in{i}_{h}", [P, C, P], F32R) for h in range(2)] for i in range(2)]
        hid = [sb(f"hid{i}", [P, F]) for i in range(2)]
        hid_col = [[sb(f"hid_col{i}_{h}", [P, FC, P], F32R) for h in range(2)] for i in range(2)]
        rows_out = [sb(f"rows_out{i}", [P, D]) for i in range(RING)]

        count = sb("count", [P, NX])
        tiles_i = sb("tiles_i", [P, NX], I32)
        tiles_s = sb("tiles_s", [P, NX], I32)
        tiles = sb("tiles", [P, NX])
        ends = sb("ends", [P, NX])
        shift = sb("shift", [P, NX])
        shift_more = sb("shift_more", [P, NX])
        skip = sb("skip", [P, NX])
        move = sb("move", [P, TOP * v.NT, NX])
        moved = sb("moved", [P, TOP * v.NT])
        tail_i = sb("tail_i", [1, NX], I32)
        step_i = sb("step_i", [1, STEPS], I32)
        step_f = sb("step_f", [1, STEPS])
        past = sb("past", [1, STEPS, NX])
        which = sb("which", [1, STEPS])
        skipped = sb("skipped", [1, STEPS])
        row_f = sb("row_f", [1, STEPS])
        real = sb("real", [1, STEPS])
        from_f = sb("from_f", [1, STEPS])
        which_f = sb("which_f", [1, STEPS])
        from_row = sb("from_row", [1, STEPS], I32)
        expert = sb("expert", [1, STEPS], I32)

        cols_ps = [v.ps(f"cols_ps{i}", [P, C, P], ctx=ctx) for i in range(2)]
        hid_ps = [v.ps(f"ehid_ps{i}", [P, 512], ctx=ctx) for i in range(2)]
        hcol_ps = [v.ps(f"hcol_ps{i}", [P, 4, P], ctx=ctx) for i in range(2)]
        out_ps = [v.ps(f"eout_ps{i}", [P, D], ctx=ctx) for i in range(2)]

        weights_in = sem("expert_weights_in")
        bias1_in = sem("expert_bias1_in")
        bias2_in = sem("expert_bias2_in")
        high_made = sem("expert_high_made")
        weights_ready = sem("expert_weights_ready")
        cols_low_ready = sem("cols_low_ready")
        hcol_low_ready = sem("hcol_low_ready")
        table_chain = sem("table_chain")
        steps_made = sem("steps_made")
        tails_ready = sem("tails_ready")
        table_ready = sem("table_ready")
        zeros_ready = sem("zeros_ready")
        tails_stored = sem("tails_stored")
        rows_loaded = [sem(f"rows_loaded{i}") for i in range(RING)]
        rows_turned = sem("erows_turned")
        cols_ready = sem("cols_ready")
        hid_made = sem("ehid_made")
        hid_ready = sem("ehid_ready")
        hid_turned = sem("ehid_turned")
        hcol_ready = sem("hcol_ready")
        out_made = sem("eout_made")
        out_ready = sem("eout_ready")
        out_stored = [sem(f"eout_stored{i}") for i in range(RING)]

        block = ctx.enter_context(nc.Block())

        @block.sync
        def _(sp):
            sp.wait_ge(tails_ready, 1)
            sp.wait_ge(zeros_ready, 1)
            for e in range(NX):
                row = sp.value_load(tail_i[0:1, e:e + 1], min_val=0, max_val=NX * REGION - P)
                sp.dma_start(v.sent[bass.ds(row, P), :], zeros[:, :]).then_inc(tails_stored, 16)
            sp.wait_ge(table_ready, 2)
            sp.wait_ge(tails_stored, 16 * NX)

            def step(k, u):
                t = k * SLOTS + u
                if inside(k, t, 0, STEPS):
                    if inside(k, t, RING, STEPS):
                        sp.wait_ge(rows_turned, t - RING + 1)
                    row = sp.value_load(from_row[0:1, bass.ds(t, 1)], min_val=0, max_val=NX * REGION - P)
                    sp.dma_start(rows_in[u % RING][:, :], v.sent[bass.ds(row, P), :]).then_inc(rows_loaded[u % RING], 16)

            run_steps(sp, SLOTS, STEPS, STEPS, step)
            for u in range(RING):
                sp.wait_ge(out_stored[u], 16 * len(range(u, STEPS, RING)))

        @block.gpsimd
        def _(pool):
            nc.gpsimd.memset(zeros[:, :], 0.0).then_inc(zeros_ready, 1)
            nc.gpsimd.iota(step_i[:, :], pattern=[[1, STEPS]], base=0, channel_multiplier=0).then_inc(steps_made, 1)
            parts = ((w1, C * F, w1_raw, v.EW1, C), (w2, FC * D, w2_raw, v.EW2, FC))
            for e in range(NX):
                for w, n, raw, given, chunks in parts:
                    pool.dma_start(raw[:, :].rearrange("p (c n) -> p c n", c=chunks),
                                   given[e].rearrange("(c p) n -> p c n", p=P)).then_inc(weights_in, 16)
                pool.wait_ge(weights_in, 16 * 2 * (e + 1))
                if e > 0:
                    for w, n, raw, given, chunks in parts:
                        nc.gpsimd.tensor_copy(w[0][:, e * n:(e + 1) * n], raw[:, :]).then_inc(high_made, 1)
                pool.wait_ge(high_made, 2 * (e + 1))
                for w, n, raw, given, chunks in parts:
                    last = nc.gpsimd.tensor_tensor(w[1][:, e * n:(e + 1) * n], raw[:, :],
                                                   w[0][:, e * n:(e + 1) * n].bitcast(F32), ALU.subtract)
                last.then_inc(weights_ready, 1)
                pool.wait_ge(weights_ready, e + 1)

        @block.scalar
        def _(act):
            act.dma_start(bias1[:, :], v.Eb1.rearrange("e f -> (e f)").partition_broadcast(P)).then_inc(bias1_in, 16)
            act.wait_ge(weights_in, 16 * 2)
            for w, n, raw in ((w1, C * F, w1_raw), (w2, FC * D, w2_raw)):
                nc.scalar.activation(w[0][:, 0:n], raw[:, :], ACT.Copy).then_inc(high_made, 1)
            act.wait_ge(rows_loaded[0], 16)
            act.dma_start(bias2[:, :], v.Eb2.rearrange("e d -> (e d)").partition_broadcast(P)).then_inc(bias2_in, 16)

            def step(k, u):
                t = k * SLOTS + u
                _, ub, tb = back(k, u, 2, SLOTS)
                if inside(k, tb, 0, STEPS):
                    act.wait_ge(hid_turned, tb + 1)
                    if inside(k, tb, 2, STEPS):
                        act.wait_ge(out_made, tb - 1)
                    nc.scalar.activation(hid_col[ub % 2][0][:, :, :], hcol_ps[ub % 2][:, 0:FC, :],
                                         ACT.Relu).then_inc(hcol_ready, 1)
                if inside(k, t, 0, STEPS):
                    act.wait_ge(rows_turned, t + 1)
                    if inside(k, t, 2, STEPS):
                        act.wait_ge(hid_made, t - 1)
                    nc.scalar.activation(cols_in[u % 2][0][:, :, :], cols_ps[u % 2][:, :, :],
                                         ACT.Copy).then_inc(cols_ready, 1)
                _, ub, tb = back(k, u, 3, SLOTS)
                if inside(k, tb, 0, STEPS):
                    act.wait_ge(out_ready, tb + 1)
                    act.dma_start(v.made[bass.ds(tb * P, P), :],
                                  rows_out[ub % RING][:, :]).then_inc(out_stored[ub % RING], 16)

            run_steps(act, SLOTS, STEPS + 3, STEPS, step)

        @block.vector
        def _(dve):
            c = Chain(dve, table_chain, 0)
            nc.vector.tensor_copy(tail_i[:, :], v.run_row[0:1, :]).then_inc(tails_ready, 1)
            c.link(nc.vector.tensor_tensor(count[:, :], v.run_row[:, :], v.region_row[:, :], ALU.subtract))
            c.link(nc.vector.tensor_scalar(tiles_i[:, :], count[:, :], float(P - 1), None, ALU.add))
            c.link(nc.vector.tensor_scalar(tiles_s[:, :], tiles_i[:, :], P.bit_length() - 1, None,
                                           ALU.arith_shift_right))
            c.link(nc.vector.tensor_copy(tiles[:, :], tiles_s[:, :]))
            c.link(nc.vector.tensor_copy(ends[:, :], tiles[:, :]))
            for e in range(1, NX):
                c.link(nc.vector.tensor_tensor(ends[:, e:e + 1], ends[:, e - 1:e], tiles[:, e:e + 1], ALU.add))
            c.link(nc.vector.tensor_tensor(shift[:, :], ends[:, :], tiles[:, :], ALU.subtract))
            c.link(nc.vector.scalar_tensor_tensor(out=shift[:, :], in0=shift[:, :], scalar=float(P),
                                                  in1=v.region_row[:, :], op0=ALU.mult, op1=ALU.subtract))
            c.link(nc.vector.tensor_copy(shift_more[:, 0:1], shift[:, 0:1]))
            c.link(nc.vector.tensor_tensor(shift_more[:, 1:], shift[:, 1:], shift[:, 0:NX - 1], ALU.subtract))
            c.link(nc.vector.tensor_scalar(skip[:, :], tiles[:, :], float(-P), float(REGION), ALU.mult, ALU.add))
            dve.wait_ge(steps_made, 1)
            c.link(nc.vector.tensor_copy(step_f[:, :], step_i[:, :]))
            c.link(nc.vector.tensor_tensor(past[:, :, :], step_f[:, :].unsqueeze(2).to_broadcast([1, STEPS, NX]),
                                           ends[0:1, :].unsqueeze(1).to_broadcast([1, STEPS, NX]), ALU.is_ge))
            c.link(nc.vector.tensor_reduce(which[:, :], past[:, :, :], AX_X, ALU.add))
            c.link(nc.vector.tensor_tensor(past[:, :, :], past[:, :, :],
                                           skip[0:1, :].unsqueeze(1).to_broadcast([1, STEPS, NX]), ALU.mult))
            c.link(nc.vector.tensor_reduce(skipped[:, :], past[:, :, :], AX_X, ALU.add))
            c.link(nc.vector.scalar_tensor_tensor(out=row_f[:, :], in0=step_f[:, :], scalar=float(P),
                                                  in1=skipped[:, :], op0=ALU.mult, op1=ALU.add))
            c.link(nc.vector.tensor_scalar(real[:, :], which[:, :], float(NX), None, ALU.is_lt))
            c.link(nc.vector.tensor_tensor(from_f[:, :], row_f[:, :], real[:, :], ALU.mult))
            c.link(nc.vector.tensor_tensor(which_f[:, :], which[:, :], real[:, :], ALU.mult))
            nc.vector.tensor_copy(from_row[:, :], from_f[:, :]).then_inc(table_ready, 1)
            nc.vector.tensor_copy(expert[:, :], which_f[:, :]).then_inc(table_ready, 1)
            dve.wait_ge(table_ready, 2)
            for rows, tiles_from, tiles_to in ((P, 0, v.NT - 1), (v.TAIL, v.NT - 1, v.NT)):
                lo, hi = TOP * tiles_from, TOP * tiles_to
                whole = [rows, hi - lo, NX]
                place = v.place[0:rows, tiles_from:tiles_to, :].rearrange("p t i -> p (t i)")
                moves = move[0:rows, lo:hi, :]
                c.link(nc.vector.tensor_tensor(moves, place.unsqueeze(2).to_broadcast(whole),
                                               v.region_row[0:rows, :].unsqueeze(1).to_broadcast(whole), ALU.is_ge))
                c.link(nc.vector.tensor_tensor(moves, moves, shift_more[0:rows, :].unsqueeze(1).to_broadcast(whole),
                                               ALU.mult))
                c.link(nc.vector.tensor_reduce(moved[0:rows, lo:hi], moves, AX_X, ALU.add))
                c.link(nc.vector.tensor_tensor(place, place, moved[0:rows, lo:hi], ALU.add))

            def expert_at(t):
                return dve.value_load(expert[0:1, bass.ds(t, 1)], min_val=0, max_val=NX - 1)

            loaded = {}

            def step(k, u):
                t = k * SLOTS + u
                two = loaded.get("one") if u else (expert_at(t - 2) if inside(k, t - 2, 0, STEPS) else None)
                one = loaded["one"] = expert_at(t - 1) if inside(k, t - 1, 0, STEPS) else None
                kb, ub, tb = back(k, u, 2, SLOTS)
                if inside(k, tb, 0, STEPS):
                    dve.wait_ge(hcol_ready, tb + 1)
                    nc.vector.scalar_tensor_tensor(out=hid_col[ub % 2][1][:, :, :], in0=hcol_ps[ub % 2][:, 0:FC, :],
                                                   scalar=0.0, in1=hid_col[ub % 2][0][:, :, :].bitcast(F32),
                                                   op0=ALU.max, op1=ALU.subtract).then_inc(hcol_low_ready, 1)
                if inside(k, t, 0, STEPS):
                    dve.wait_ge(cols_ready, t + 1)
                    nc.vector.tensor_tensor(cols_in[u % 2][1][:, :, :], cols_ps[u % 2][:, :, :],
                                            cols_in[u % 2][0][:, :, :].bitcast(F32),
                                            ALU.subtract).then_inc(cols_low_ready, 1)
                kb, ub, tb = back(k, u, 1, SLOTS)
                if inside(k, tb, 0, STEPS):
                    if not inside(k, tb, 1, STEPS):
                        dve.wait_ge(bias1_in, 16)
                    dve.wait_ge(hid_made, tb + 1)
                    if inside(k, tb, 2, STEPS):
                        dve.wait_ge(hid_turned, tb - 1)
                    nc.vector.tensor_tensor(hid[ub % 2][:, :], hid_ps[ub % 2][:, 0:F], bias1[:, bass.ds(one * F, F)],
                                            ALU.add).then_inc(hid_ready, 1)
                kb, ub, tb = back(k, u, 2, SLOTS)
                if inside(k, tb, 0, STEPS):
                    if not inside(k, tb, 1, STEPS):
                        dve.wait_ge(bias2_in, 16)
                    dve.wait_ge(out_made, tb + 1)
                    if inside(k, tb, RING, STEPS):
                        dve.wait_ge(out_stored[ub % RING], 16 * turn(kb, ub))
                    nc.vector.tensor_tensor(rows_out[ub % RING][:, :], out_ps[ub % 2][:, :], bias2[:, bass.ds(two * D, D)],
                                            ALU.add).then_inc(out_ready, 1)

            run_steps(dve, SLOTS, STEPS + 2, STEPS, step)

        @block.tensor
        def _(pe):
            pe.wait_ge(table_ready, 2)

            def expert_at(t):
                return pe.value_load(expert[0:1, bass.ds(t, 1)], min_val=0, max_val=NX - 1)

            loaded = {}

            def three_products(to, cols, w, e, chunks, n):
                passes = [(c, a, b) for c in range(chunks) for a, b in ((0, 0), (0, 1), (1, 0))]
                for i, (c, a, b) in enumerate(passes):
                    last = nc.tensor.matmul(to, cols[a][:, c, :], w[b][:, bass.ds(e * (chunks * n) + c * n, n)],
                                            start=(i == 0), stop=(i == len(passes) - 1))
                return last

            def step(k, u):
                t = k * SLOTS + u
                two = loaded.get("one") if u else (expert_at(t - 2) if inside(k, t - 2, 0, STEPS) else None)
                one = loaded["one"] = expert_at(t - 1) if inside(k, t - 1, 0, STEPS) else None
                _, ub, tb = back(k, u, 2, SLOTS)
                if inside(k, tb, 0, STEPS):
                    pe.wait_ge(hid_ready, tb + 1)
                    if inside(k, tb, 2, STEPS):
                        pe.wait_ge(hcol_low_ready, tb - 1)
                    for c in range(FC):
                        last = nc.tensor.transpose(hcol_ps[ub % 2][:, c, :], hid[ub % 2][:, c * P:(c + 1) * P],
                                                   v.ident[:, :])
                    last.then_inc(hid_turned, 1)
                if inside(k, t, 0, STEPS):
                    pe.wait_ge(rows_loaded[u % RING], 16 * (turn(k, u) + 1))
                    if inside(k, t, 2, STEPS):
                        pe.wait_ge(cols_low_ready, t - 1)
                    for c in range(C):
                        last = nc.tensor.transpose(cols_ps[u % 2][:, c, :], rows_in[u % RING][:, c * P:(c + 1) * P],
                                                   v.ident[:, :])
                    last.then_inc(rows_turned, 1)
                _, ub, tb = back(k, u, 1, SLOTS)
                if inside(k, tb, 0, STEPS):
                    pe.wait_ge(weights_ready, one + 1)
                    pe.wait_ge(cols_low_ready, tb + 1)
                    if inside(k, tb, 2, STEPS):
                        pe.wait_ge(hid_ready, tb - 1)
                    three_products(hid_ps[ub % 2][:, 0:F], cols_in[ub % 2], w1, one, C, F).then_inc(hid_made, 1)
                _, ub, tb = back(k, u, 2, SLOTS)
                if inside(k, tb, 0, STEPS):
                    pe.wait_ge(hcol_low_ready, tb + 1)
                    if inside(k, tb, 2, STEPS):
                        pe.wait_ge(out_ready, tb - 1)
                    three_products(out_ps[ub % 2][:, :], hid_col[ub % 2], w2, two, FC, D).then_inc(out_made, 1)

            run_steps(pe, SLOTS, STEPS + 2, STEPS, step)


def combine(nc, v):
    N, D, NT = v.N, v.D, v.NT
    sem = v.sem
    SLOTS = 4

    with ExitStack() as ctx:
        def sb(name, shape, dt=F32):
            return v.sb(name, shape, dt, ctx=ctx)

        x2 = [sb(f"x2_in{i}", [P, D]) for i in range(SLOTS)]
        got = [sb(f"got{i}", [P, TOP, D]) for i in range(SLOTS)]
        one = [sb(f"one{i}", [P, D]) for i in range(2)]
        final = [sb(f"final{i}", [P, D]) for i in range(SLOTS)]
        index = [sb(f"place_int{i}", [P, TOP], I32) for i in range(SLOTS)]

        x2_loaded = [sem(f"x2_loaded{i}") for i in range(SLOTS)]
        index_ready = sem("place_int_ready")
        fetched = [sem(f"fetched{i}") for i in range(SLOTS)]
        one_ready = sem("one_ready")
        final_ready = sem("final_ready")
        out_stored = [sem(f"out_stored{i}") for i in range(SLOTS)]

        block = ctx.enter_context(nc.Block())

        @block.sync
        def _(sp):
            def load(k, u, t):
                r = v.rows_of(t)
                sp.dma_start(x2[u][0:r, :], v.resid[bass.ds(t * P, r), :]).then_inc(x2_loaded[u], 16)

            for t in range(SLOTS):
                load(0, t, t)

            def step(k, u):
                t = k * SLOTS + u
                r = v.rows_of(t)
                sp.wait_ge(final_ready, t + 1)
                sp.dma_start(v.out[bass.ds(t * P, r), :], final[u][0:r, :]).then_inc(out_stored[u], 16)
                if inside(k, t + SLOTS, 0, NT):
                    load(k + 1, u, t + SLOTS)

            run_steps(sp, SLOTS, NT, NT - 1 - SLOTS, step)
            for u in range(SLOTS):
                sp.wait_ge(out_stored[u], 16 * len(range(u, NT, SLOTS)))

        @block.scalar
        def _(act):
            def step(k, u):
                t = k * SLOTS + u
                r = v.rows_of(t)
                if inside(k, t, SLOTS, NT):
                    act.wait_ge(fetched[u], 16 * TOP * k)
                nc.scalar.activation(index[u][0:r, :], v.place[0:r, bass.ds(t, 1), :].rearrange("p t i -> p (t i)"),
                                     ACT.Copy).then_inc(index_ready, 1)

            run_steps(act, SLOTS, NT, NT - 1, step)

        @block.gpsimd
        def _(pool):
            def step(k, u):
                t = k * SLOTS + u
                r = v.rows_of(t)
                pool.wait_ge(index_ready, t + 1)
                if inside(k, t, SLOTS, NT):
                    pool.wait_ge(final_ready, t - SLOTS + 1)
                stand_for(pool, v.waits_passed)
                for i in range(TOP):
                    nc.gpsimd.indirect_dma_start(
                        out=got[u][0:r, i, :], out_offset=None, in_=v.made[:, :],
                        in_offset=bass.IndirectOffsetOnAxis(ap=index[u][0:r, i:i + 1], axis=0)
                    ).then_inc(fetched[u], 16)

            run_steps(pool, SLOTS, NT, NT - 1, step)

        @block.vector
        def _(dve):
            def step(k, u):
                t = k * SLOTS + u
                r = v.rows_of(t)
                dve.wait_ge(x2_loaded[u], 16 * (k + 1))
                dve.wait_ge(fetched[u], 16 * TOP * (k + 1))

                def w(i):
                    return v.weight[0:r, bass.ds(t, 1), i]

                nc.vector.scalar_tensor_tensor(out=one[u % 2][0:r, :], in0=got[u][0:r, 0, :], scalar=w(0),
                                               in1=x2[u][0:r, :], op0=ALU.mult, op1=ALU.add).then_inc(one_ready, 1)
                dve.wait_ge(one_ready, t + 1)
                if inside(k, t, SLOTS, NT):
                    dve.wait_ge(out_stored[u], 16 * k)
                nc.vector.scalar_tensor_tensor(out=final[u][0:r, :], in0=got[u][0:r, 1, :], scalar=w(1),
                                               in1=one[u % 2][0:r, :], op0=ALU.mult,
                                               op1=ALU.add).then_inc(final_ready, 1)

            run_steps(dve, SLOTS, NT, NT - 1, step)


_INS = ["x", "src", "dst", "L0_gnn_W1", "L0_gnn_b1", "L0_gnn_W2", "L0_gnn_b2", "L0_ffn_Wr", "L0_ffn_br",
        "L0_ffn_W1", "L0_ffn_b1", "L0_ffn_W2", "L0_ffn_b2"]


def kernel(**inputs):
    import numpy as _np
    import concourse.bacc as _bacc
    from concourse import mybir as _mybir
    from concourse.bass_utils import run_bass_kernel_spmd as _run

    nc = _bacc.Bacc("TRN2", target_bir_lowering=False, num_devices=1)
    arrays, args = {}, []
    for name in _INS:
        a = _np.ascontiguousarray(inputs[name])
        arrays[f"in_{name}_dram"] = a
        args.append(nc.dram_tensor(f"in_{name}_dram", a.shape, _mybir.dt.from_np(a.dtype), kind="ExternalInput").ap())
    shape = tuple(inputs["x"].shape)
    args.append(nc.dram_tensor("out_0_dram", shape, _mybir.dt.float32, kind="ExternalOutput").ap())
    gnn_moe_kernel(nc, *args)
    r = _run(nc, [arrays], core_ids=[0])
    return r.results[0]["out_0_dram"]
```
